# Optimizing a Trainium2 kernel written in Bass

```python
import numpy as np
import jax
import jax.numpy as jnp

def _softmax(x, axis=-1):
    return jax.nn.softmax(x, axis=axis)

def _gelu(x):
    return jax.nn.gelu(x, approximate=True)

def _silu(x):
    return jax.nn.silu(x)

def _sigmoid(x):
    return jax.nn.sigmoid(x)

def _layernorm(x, axis=-1, eps=1e-05):
    m = jnp.mean(x, axis=axis, keepdims=True)
    v = jnp.var(x, axis=axis, keepdims=True)
    return (x - m) / jnp.sqrt(v + eps)

def _scatter_add(tgt, idx, src, axis=0):
    return tgt.at[idx].add(src)

def _segment_sum(src, seg, n):
    return jax.ops.segment_sum(src, seg, n)
kernel_name = 'mk_audio_tower_d2_tok_audfeat256_r4_acc360'

def setup_inputs(seed: int=0):
    np.random.seed(seed)
    _w = jnp.asarray

    def _rec_inputs():
        import jax
        import jax.numpy as jnp
        _rk = jax.random.key(seed)
        x = 7.22013e-05 + 1.00017 * jax.random.normal(jax.random.fold_in(_rk, 1), (128, 125, 128), jnp.float32)
        return x
    x = _rec_inputs()

    def _L0_tok_setup():
        import jax, jax.numpy as jnp
        import numpy as np
        K = 9
        EPS = 1e-05

        def _conv1d_valid(x, w):
            return jax.lax.conv_general_dilated(x, w, window_strides=(1,), padding='VALID', dimension_numbers=('NWC', 'WIO', 'NWC'))
        key = jax.random.key(seed)
        k1, k2 = jax.random.split(key)
        B, L, Cin, F = (16, 1024, 128, 64)
        inputs = jax.random.normal(k1, (B, L, Cin), dtype=jnp.float32)
        kernel = jax.random.normal(k2, (K, Cin, F), dtype=jnp.float32) * 0.05
        kernel = kernel / jnp.sqrt(jnp.sum(kernel ** 2, axis=(0, 1), keepdims=True))
        scale = jnp.full((1, 1, 1), 10.0, dtype=jnp.float32)
        bias = jnp.zeros((F,), dtype=jnp.float32)
        tau = jnp.full((1, 1, 1), np.sqrt(K) * 0.75, dtype=jnp.float32)
        alpha = jnp.full((1, 1, 1), 3.0, dtype=jnp.float32)
        return {'inputs': inputs, 'kernel': kernel, 'scale': scale, 'bias': bias, 'tau': tau, 'alpha': alpha}
    _L0_tok_all = _L0_tok_setup()
    _L0_tok_in = {k: v for k, v in _L0_tok_all.items() if k in ('kernel', 'scale', 'bias', 'tau', 'alpha')}
    del _L0_tok_all

    def _L0_attn_setup():
        import jax, jax.numpy as jnp
        import numpy as np
        key = jax.random.key(seed)
        k1, k2, k3 = jax.random.split(key, 3)
        b, n_t, n, n_h = (8, 256, 64, 8)
        s = jax.random.normal(k1, (b, n_t, n), dtype=jnp.float32)
        Q = jax.random.normal(k2, (n_h, n, n), dtype=jnp.float32) * 0.02
        E = jax.random.normal(k3, (n_h, n, n), dtype=jnp.float32) * 0.02
        return {'s': s, 'Q': Q, 'E': E}
    _L0_attn_all = _L0_attn_setup()
    _L0_attn_in = {k: v for k, v in _L0_attn_all.items() if k in ('Q', 'E')}
    del _L0_attn_all

    def _L0_ffn_setup():
        import jax, jax.numpy as jnp
        import numpy as np
        B, A = (1024, 8)
        IN, OUT = (64, 64)
        SH1, SH2 = (64, 128)
        EH1, EH2 = (128, 64)
        E, TOPK = (4, 2)

        def _shared_mlp(x, W1, b1, W2, b2, W3, b3):
            h = jax.nn.relu(x @ W1 + b1)
            h = jax.nn.relu(h @ W2 + b2)
            return h @ W3 + b3

        def _experts_mlp(x, eW1, eb1, eW2, eb2, eW3, eb3):
            h = jax.nn.relu(jnp.einsum('baf,efh->ebah', x, eW1) + eb1[:, None, None, :])
            h = jax.nn.relu(jnp.einsum('ebah,ehg->ebag', h, eW2) + eb2[:, None, None, :])
            o = jnp.einsum('ebag,ego->ebao', h, eW3) + eb3[:, None, None, :]
            return jnp.moveaxis(o, 0, -1)
        key = jax.random.key(seed)
        ks = jax.random.split(key, 16)
        s = 0.05
        return {'x': jax.random.normal(ks[0], (B, A, IN), jnp.float32), 'sW1': jax.random.normal(ks[1], (IN, SH1), jnp.float32) * s, 'sb1': jnp.zeros((SH1,), jnp.float32), 'sW2': jax.random.normal(ks[2], (SH1, SH2), jnp.float32) * s, 'sb2': jnp.zeros((SH2,), jnp.float32), 'sW3': jax.random.normal(ks[3], (SH2, OUT), jnp.float32) * s, 'sb3': jnp.zeros((OUT,), jnp.float32), 'eW1': jax.random.normal(ks[4], (E, IN, EH1), jnp.float32) * s, 'eb1': jnp.zeros((E, EH1), jnp.float32), 'eW2': jax.random.normal(ks[5], (E, EH1, EH2), jnp.float32) * s, 'eb2': jnp.zeros((E, EH2), jnp.float32), 'eW3': jax.random.normal(ks[6], (E, EH2, OUT), jnp.float32) * s, 'eb3': jnp.zeros((E, OUT), jnp.float32), 'gW': jax.random.normal(ks[7], (IN, E), jnp.float32) * s, 'gb': jnp.zeros((E,), jnp.float32)}
    _L0_ffn_all = _L0_ffn_setup()
    _L0_ffn_in = {k: v for k, v in _L0_ffn_all.items() if k in ('sW1', 'sb1', 'sW2', 'sb2', 'sW3', 'sb3', 'eW1', 'eb1', 'eW2', 'eb2', 'eW3', 'eb3', 'gW', 'gb')}
    del _L0_ffn_all

    def _L1_attn_setup():
        import jax, jax.numpy as jnp
        import numpy as np
        DIM = 64
        WS = 64
        H = 8
        HD = DIM // H
        SCALE = HD ** (-0.5)
        key = jax.random.key(seed)
        k1, k2, k3, k4 = jax.random.split(key, 4)
        B, L = (8, 4096)
        x = jax.random.normal(k1, (B, L, DIM), dtype=jnp.float32)
        w_qkv = jax.random.normal(k2, (3 * DIM, DIM), dtype=jnp.float32) * DIM ** (-0.5)
        w_proj = jax.random.normal(k3, (DIM, DIM), dtype=jnp.float32) * DIM ** (-0.5)
        b_proj = jnp.zeros((DIM,), dtype=jnp.float32)
        rel_bias = jax.random.normal(k4, (2 * WS - 1,), dtype=jnp.float32) * 0.02
        return {'x': x, 'w_qkv': w_qkv, 'w_proj': w_proj, 'b_proj': b_proj, 'rel_bias': rel_bias}
    _L1_attn_all = _L1_attn_setup()
    _L1_attn_in = {k: v for k, v in _L1_attn_all.items() if k in ('w_qkv', 'w_proj', 'b_proj', 'rel_bias')}
    del _L1_attn_all

    def _L1_ffn_setup():
        import jax, jax.numpy as jnp
        import numpy as np
        B, S, H, F, E, K = (8, 1024, 64, 128, 16, 2)
        EPS = 1e-05
        key = jax.random.key(seed)
        ks = jax.random.split(key, 9)
        sc = 0.02
        return {'x': jax.random.normal(ks[0], (B, S, H), dtype=jnp.float32), 'gate_w': jax.random.normal(ks[1], (H, E), dtype=jnp.float32) * sc, 'gate_b': jnp.zeros((E,), dtype=jnp.float32), 'w1': jax.random.normal(ks[2], (E, H, F), dtype=jnp.float32) * sc, 'b1': jnp.zeros((E, F), dtype=jnp.float32), 'w2': jax.random.normal(ks[3], (E, F, H), dtype=jnp.float32) * sc, 'b2': jnp.zeros((E, H), dtype=jnp.float32), 'gamma': jnp.ones((H,), dtype=jnp.float32), 'beta': jnp.zeros((H,), dtype=jnp.float32)}
    _L1_ffn_all = _L1_ffn_setup()
    _L1_ffn_in = {k: v for k, v in _L1_ffn_all.items() if k in ('gate_w', 'gate_b', 'w1', 'b1', 'w2', 'b2', 'gamma', 'beta')}
    del _L1_ffn_all
    return {'x': x, 'L0_tok_kernel': _L0_tok_in['kernel'], 'L0_tok_scale': _L0_tok_in['scale'], 'L0_tok_bias': _L0_tok_in['bias'], 'L0_tok_tau': _L0_tok_in['tau'], 'L0_tok_alpha': _L0_tok_in['alpha'], 'L0_attn_Q': _L0_attn_in['Q'], 'L0_attn_E': _L0_attn_in['E'], 'L0_ffn_sW1': _L0_ffn_in['sW1'], 'L0_ffn_sb1': _L0_ffn_in['sb1'], 'L0_ffn_sW2': _L0_ffn_in['sW2'], 'L0_ffn_sb2': _L0_ffn_in['sb2'], 'L0_ffn_sW3': _L0_ffn_in['sW3'], 'L0_ffn_sb3': _L0_ffn_in['sb3'], 'L0_ffn_eW1': _L0_ffn_in['eW1'], 'L0_ffn_eb1': _L0_ffn_in['eb1'], 'L0_ffn_eW2': _L0_ffn_in['eW2'], 'L0_ffn_eb2': _L0_ffn_in['eb2'], 'L0_ffn_eW3': _L0_ffn_in['eW3'], 'L0_ffn_eb3': _L0_ffn_in['eb3'], 'L0_ffn_gW': _L0_ffn_in['gW'], 'L0_ffn_gb': _L0_ffn_in['gb'], 'L1_attn_w_qkv': _L1_attn_in['w_qkv'], 'L1_attn_w_proj': _L1_attn_in['w_proj'], 'L1_attn_b_proj': _L1_attn_in['b_proj'], 'L1_attn_rel_bias': _L1_attn_in['rel_bias'], 'L1_ffn_gate_w': _L1_ffn_in['gate_w'], 'L1_ffn_gate_b': _L1_ffn_in['gate_b'], 'L1_ffn_w1': _L1_ffn_in['w1'], 'L1_ffn_b1': _L1_ffn_in['b1'], 'L1_ffn_w2': _L1_ffn_in['w2'], 'L1_ffn_b2': _L1_ffn_in['b2'], 'L1_ffn_gamma': _L1_ffn_in['gamma'], 'L1_ffn_beta': _L1_ffn_in['beta']}

def reference(x, L0_tok_kernel, L0_tok_scale, L0_tok_bias, L0_tok_tau, L0_tok_alpha, L0_attn_Q, L0_attn_E, L0_ffn_sW1, L0_ffn_sb1, L0_ffn_sW2, L0_ffn_sb2, L0_ffn_sW3, L0_ffn_sb3, L0_ffn_eW1, L0_ffn_eb1, L0_ffn_eW2, L0_ffn_eb2, L0_ffn_eW3, L0_ffn_eb3, L0_ffn_gW, L0_ffn_gb, L1_attn_w_qkv, L1_attn_w_proj, L1_attn_b_proj, L1_attn_rel_bias, L1_ffn_gate_w, L1_ffn_gate_b, L1_ffn_w1, L1_ffn_b1, L1_ffn_w2, L1_ffn_b2, L1_ffn_gamma, L1_ffn_beta):
    import jax
    import jax.numpy as jnp

    def _L0_tok_ref(inputs, kernel, scale, bias, tau, alpha):
        import jax, jax.numpy as jnp
        import numpy as np
        K = 9
        EPS = 1e-05

        def _conv1d_valid(x, w):
            return jax.lax.conv_general_dilated(x, w, window_strides=(1,), padding='VALID', dimension_numbers=('NWC', 'WIO', 'NWC'))
        dot = _conv1d_valid(inputs, kernel)
        sq_sum = jnp.sum(inputs ** 2, axis=-1, keepdims=True)
        ones_k = jnp.ones((K, 1, 1), dtype=inputs.dtype)
        patch_energy = _conv1d_valid(sq_sum, ones_k)
        patch_norms = jnp.sqrt(patch_energy + EPS)
        cosine_sim = dot / (patch_norms + EPS)
        gate = jax.nn.sigmoid(alpha * (patch_norms - tau))
        return scale * (cosine_sim * gate) + bias

    def _L0_attn_ref(s, Q, E):
        import jax, jax.numpy as jnp
        import numpy as np
        n_t = s.shape[1]
        qs = jnp.einsum('bti,hij->bhtj', s, Q)
        Omega = jnp.einsum('bhtj,buj->bhtu', qs, s)
        mask = jnp.tril(jnp.ones((n_t, n_t), dtype=s.dtype))
        Omega = Omega * mask
        es = jnp.einsum('hij,buj->bhui', E, s)
        r = jnp.einsum('bhtu,bhui->bti', Omega, es)
        return r

    def _L0_ffn_ref(x, sW1, sb1, sW2, sb2, sW3, sb3, eW1, eb1, eW2, eb2, eW3, eb3, gW, gb):
        import jax, jax.numpy as jnp
        import numpy as np
        B, A = (1024, 8)
        IN, OUT = (64, 64)
        SH1, SH2 = (64, 128)
        EH1, EH2 = (128, 64)
        E, TOPK = (4, 2)

        def _shared_mlp(x, W1, b1, W2, b2, W3, b3):
            h = jax.nn.relu(x @ W1 + b1)
            h = jax.nn.relu(h @ W2 + b2)
            return h @ W3 + b3

        def _experts_mlp(x, eW1, eb1, eW2, eb2, eW3, eb3):
            h = jax.nn.relu(jnp.einsum('baf,efh->ebah', x, eW1) + eb1[:, None, None, :])
            h = jax.nn.relu(jnp.einsum('ebah,ehg->ebag', h, eW2) + eb2[:, None, None, :])
            o = jnp.einsum('ebag,ego->ebao', h, eW3) + eb3[:, None, None, :]
            return jnp.moveaxis(o, 0, -1)
        all_out = _experts_mlp(x, eW1, eb1, eW2, eb2, eW3, eb3)
        shared = _shared_mlp(x, sW1, sb1, sW2, sb2, sW3, sb3)
        gates = jax.nn.softmax(x @ gW + gb, axis=-1)
        topv, topi = jax.lax.top_k(gates, TOPK)
        topw = jax.nn.softmax(topv, axis=-1)
        sel = jnp.take_along_axis(all_out, topi[:, :, None, :], axis=-1)
        gated = jnp.sum(sel * topw[:, :, None, :], axis=-1)
        return shared + gated

    def _L1_attn_ref(x, w_qkv, w_proj, b_proj, rel_bias):
        import jax, jax.numpy as jnp
        import numpy as np
        DIM = 64
        WS = 64
        H = 8
        HD = DIM // H
        SCALE = HD ** (-0.5)
        B, L, C = x.shape
        pad_len = (WS - L % WS) % WS
        if pad_len > 0:
            x = jnp.pad(x, ((0, 0), (0, pad_len), (0, 0)))
        padded_L = x.shape[1]
        nw = padded_L // WS
        xw = x.reshape(B, nw, WS, C)
        qkv = jnp.einsum('bnwc,oc->bnwo', xw, w_qkv)
        qkv = qkv.reshape(B, nw, WS, 3, H, HD)
        q = jnp.transpose(qkv[..., 0, :, :], (0, 1, 3, 2, 4))
        k = jnp.transpose(qkv[..., 1, :, :], (0, 1, 3, 2, 4))
        v = jnp.transpose(qkv[..., 2, :, :], (0, 1, 3, 2, 4))
        attn = jnp.einsum('bnhqd,bnhkd->bnhqk', q, k) * SCALE
        pos = jnp.arange(WS)
        rel_idx = pos[None, :] - pos[:, None] + WS - 1
        attn = attn + rel_bias[rel_idx]
        attn = jax.nn.softmax(attn, axis=-1)
        out = jnp.einsum('bnhqk,bnhkd->bnhqd', attn, v)
        out = jnp.transpose(out, (0, 1, 3, 2, 4)).reshape(B, nw, WS, C)
        out = jnp.einsum('bnwc,oc->bnwo', out, w_proj) + b_proj
        out = out.reshape(B, padded_L, C)
        if pad_len > 0:
            out = out[:, :L, :]
        return out

    def _L1_ffn_ref(x, gate_w, gate_b, w1, b1, w2, b2, gamma, beta):
        import jax, jax.numpy as jnp
        import numpy as np
        B, S, H, F, E, K = (8, 1024, 64, 128, 16, 2)
        EPS = 1e-05
        gate_logits = x @ gate_w + gate_b
        topk_vals, topk_idx = jax.lax.top_k(gate_logits, K)
        topk_w = jax.nn.softmax(topk_vals, axis=-1)
        h = jax.nn.relu(jnp.einsum('bsh,ehf->bsef', x, w1) + b1)
        expert_out = jnp.einsum('bsef,efh->bseh', h, w2) + b2
        sel = jnp.take_along_axis(expert_out, topk_idx[:, :, :, None], axis=2)
        moe = jnp.sum(topk_w[..., None] * sel, axis=2)
        y = x + moe
        mu = jnp.mean(y, axis=-1, keepdims=True)
        var = jnp.var(y, axis=-1, keepdims=True)
        return (y - mu) / jnp.sqrt(var + EPS) * gamma + beta
    h = _L0_tok_ref(x, L0_tok_kernel, L0_tok_scale, L0_tok_bias, L0_tok_tau, L0_tok_alpha)
    h = h + _L0_attn_ref(_layernorm(h, axis=-1), L0_attn_Q, L0_attn_E)
    h = h + _L0_ffn_ref(_layernorm(h, axis=-1), L0_ffn_sW1, L0_ffn_sb1, L0_ffn_sW2, L0_ffn_sb2, L0_ffn_sW3, L0_ffn_sb3, L0_ffn_eW1, L0_ffn_eb1, L0_ffn_eW2, L0_ffn_eb2, L0_ffn_eW3, L0_ffn_eb3, L0_ffn_gW, L0_ffn_gb)
    h = h + _L1_attn_ref(_layernorm(h, axis=-1), L1_attn_w_qkv, L1_attn_w_proj, L1_attn_b_proj, L1_attn_rel_bias)
    h = h + _L1_ffn_ref(_layernorm(h, axis=-1), L1_ffn_gate_w, L1_ffn_gate_b, L1_ffn_w1, L1_ffn_b1, L1_ffn_w2, L1_ffn_b2, L1_ffn_gamma, L1_ffn_beta)
    return h

_drawn_inputs = setup_inputs


def setup_inputs(seed=0):
    import zlib

    import numpy as np

    out = dict(_drawn_inputs(seed))
    spreads = {'L0_tok_bias': (0.0, 0.1),
     'L0_ffn_sb1': (0.0, 0.8),
     'L0_ffn_sb2': (0.0, 0.8),
     'L0_ffn_sb3': (0.0, 2.0),
     'L0_ffn_eb1': (0.0, 0.8),
     'L0_ffn_eb2': (0.0, 0.8),
     'L0_ffn_eb3': (0.0, 2.0),
     'L0_ffn_gb': (0.0, 0.8),
     'L1_attn_b_proj': (0.0, 2.0),
     'L1_ffn_gate_b': (0.0, 2.0),
     'L1_ffn_b1': (0.0, 2.0),
     'L1_ffn_b2': (0.0, 2.0),
     'L1_ffn_gamma': (1.0, 0.6),
     'L1_ffn_beta': (0.0, 2.0)}
    factors = {'L0_ffn_sW1': 8.0,
     'L0_ffn_sW2': 8.0,
     'L0_ffn_sW3': 6.608,
     'L0_ffn_eW1': 8.0,
     'L0_ffn_eW2': 8.0,
     'L0_ffn_eW3': 8.0,
     'L0_ffn_gW': 8.0,
     'L1_attn_rel_bias': 200.0,
     'L1_ffn_gate_w': 7.646,
     'L1_ffn_w1': 30.447,
     'L1_ffn_w2': 8.0}
    for name, (base, spread) in spreads.items():
        noise = np.random.default_rng([zlib.crc32(name.encode()), seed]).standard_normal(out[name].shape)
        drawn = base * np.exp(spread * noise) if base else spread * noise
        out[name] = jnp.asarray(drawn.astype(out[name].dtype))
    for name, factor in factors.items():
        out[name] = (out[name] * factor).astype(out[name].dtype)
    return out
```

```python
from contextlib import ExitStack

import numpy as np
import concourse.bass as bass
from concourse import mybir

F32 = mybir.dt.float32
F32R = mybir.dt.float32r
ALU = mybir.AluOpType
ACT = mybir.ActivationFunctionType
AX = mybir.AxisListType.X

B, LX, CIN, TAPS, F = 128, 125, 128, 9, 64
L = LX - TAPS + 1
G = 4
NG = B // G
N = G * L
GF = G * F
NH0 = 8
NP0 = NH0 // 2
E0, E1 = 4, 16
WS, NH1, HD = 64, 8, 8
NW = 2
W1N = L - WS
EPS = 1e-5
BIG = 3.0e38
TP = (TAPS + 1) // 2
LC = L + 1
A_, B_, C_, D_, E_ = range(5)
STAGES = 5

SPLIT = {"conv": TP * 128, "q0": NH0 * F, "w1c": (E0 + 1) * 128, "wq": 128, "wk": 128, "w1e": E1 * 128}
PLAIN = {"ident": 128, "causal": L, "band": L, "e0": NP0 * F, "gwc": E0, "w2c": E0 * F, "w2s": 128,
         "w3c": 3 * F, "eb3": F, "wv": 2 * F, "fold": 128, "wp": F, "ones_bd": 32, "gwe": E1, "w2e": E1 * F, "b2e": F,
         "bias_conv": F, "gbc": E0, "gbe": E1, "gamma": F, "beta": F, "rank_c": E0, "rank_e": E1,
         "b1c": E0 + 1, "b2c": 3, "b3c": 1, "bp": 1, "b1e": E1, "window": 2, "head": NH1,
         "alpha": 1, "tau": 1, "scale": 1}
EXACT = {"sel_c": E0 * F, "sel_e": E1, "query": 128, "rel": NH1 * WS}


def offsets(widths):
    at, out = 0, {}
    for name, n in widths.items():
        out[name] = (at, n)
        at += n
    return out, at


SPLIT_AT, NSPLIT = offsets(SPLIT)
PLAIN_AT, NPLAIN = offsets(PLAIN)
EXACT_AT, NEXACT = offsets(EXACT)


def merged(*threads):
    keyed = [((i + 0.5) / len(t), n, s) for n, t in enumerate(threads) for i, s in enumerate(t)]
    return [s for _, _, s in sorted(keyed)]


def norm_steps(s):
    return [("center", s, 0), ("variance", s, 0), ("normalise", s, 0), ("to_features", s, 0)]


STEPS = {
    A_: [("conv_load", A_, 0), ("conv", A_, 0), ("conv_fold", A_, 0), ("conv_out", A_, 0)],
    B_: norm_steps(B_) + [("keys", B_, 0)] + [("query", B_, p) for p in range(NP0)]
        + [x for b in range(G) for x in (("omega", B_, b), ("zed", B_, b))] + [("r", B_, 0), ("r_out", B_, 0)],
    C_: norm_steps(C_) + [("gate", C_, 0), ("h1_shared", C_, 0), ("soft", C_, 0), ("h1", C_, 0), ("top", C_, 0),
                          ("h1", C_, 1), ("h1", C_, 2), ("h1", C_, 3), ("weights", C_, 0), ("h2", C_, 0),
                          ("h2", C_, 1), ("h2_shared", C_, 0), ("mlp_out", C_, 0), ("r_out", C_, 0)],
    D_: norm_steps(D_) + [("window_q", D_, 0), ("window_k", D_, 0), ("window_v", D_, 0), ("score", D_, 0),
                          ("flip", D_, 0), ("score", D_, 1), ("mix", D_, 0), ("flip", D_, 1), ("score", D_, 2),
                          ("mix", D_, 1), ("flip", D_, 2), ("score", D_, 3), ("mix", D_, 2), ("flip", D_, 3),
                          ("mix", D_, 3), ("project", D_, 0), ("r_out", D_, 0)],
    E_: norm_steps(E_) + [("gate", E_, 0), ("top", E_, 0), ("weights", E_, 0)]
        + [x for j in range(E1 // 2) for x in (("expert_in", E_, j), ("expert_out", E_, j))]
        + [("expert_last", E_, 0), ("residual", E_, 0), ("center2", E_, 0), ("variance2", E_, 0),
           ("normalise2", E_, 0)],
}


ORDER = {
    "pe": (
        "D.to_features.0 D.window_q.0 D.window_k.0 E.to_features.0 D.window_v.0 B.to_features.0 E.gate.0 B.keys.0 "
        "B.query.0 D.score.0 B.query.1 B.query.2 D.flip.0 D.score.1 E.weights.0 D.mix.0 B.query.3 E.expert_in.0 "
        "D.flip.1 E.expert_out.0 D.score.2 E.expert_in.1 D.mix.1 B.omega.0 E.expert_out.1 D.flip.2 D.score.3 "
        "B.zed.0 D.mix.2 E.expert_in.2 B.omega.1 D.flip.3 E.expert_out.2 D.mix.3 B.zed.1 E.expert_in.3 "
        "D.project.0 B.omega.2 E.expert_out.3 E.expert_in.4 B.zed.2 E.expert_out.4 D.r_out.0 E.expert_in.5 "
        "C.to_features.0 B.omega.3 E.expert_out.5 C.gate.0 C.h1_shared.0 E.expert_in.6 C.h1.0 C.h1.1 B.zed.3 "
        "E.expert_out.6 E.expert_in.7 B.r.0 C.h1.2 C.h1.3 B.r_out.0 E.expert_out.7 A.conv_load.0 C.weights.0 "
        "E.expert_last.0 C.h2.0 E.residual.0 A.conv.0 C.h2.1 C.h2_shared.0 A.conv_out.0 C.mlp_out.0 C.r_out.0 "
    ),
    "act": (
        "D.center.0 E.center.0 D.normalise.0 B.center.0 E.normalise.0 D.to_features.0 B.normalise.0 D.window_q.0 "
        "D.window_k.0 E.to_features.0 B.to_features.0 B.keys.0 E.top.0 B.query.0 D.window_v.0 B.query.1 D.score.0 "
        "D.flip.0 E.weights.0 D.score.1 B.query.2 E.expert_in.0 B.query.3 D.flip.1 E.expert_in.1 D.score.2 "
        "D.flip.2 B.zed.0 D.score.3 E.expert_in.2 D.flip.3 B.zed.1 E.expert_in.3 C.center.0 D.project.0 "
        "E.expert_in.4 C.normalise.0 B.zed.2 E.expert_in.5 C.to_features.0 C.h1_shared.0 C.soft.0 E.expert_in.6 "
        "C.h1.0 B.zed.3 E.expert_in.7 C.top.0 C.h1.1 B.r.0 C.h1.2 C.h1.3 C.weights.0 A.conv_load.0 "
        "E.expert_last.0 C.h2.0 E.center2.0 A.conv_fold.0 C.h2.1 C.h2_shared.0 C.mlp_out.0 "
    ),
    "dve": (
        "D.center.0 E.center.0 D.variance.0 E.variance.0 B.center.0 D.normalise.0 E.normalise.0 B.variance.0 "
        "B.normalise.0 E.gate.0 E.top.0 E.weights.0 D.score.0 D.score.1 D.mix.0 E.expert_in.0 E.expert_out.0 "
        "D.score.2 E.expert_in.1 D.mix.1 B.omega.0 E.expert_out.1 D.score.3 D.mix.2 E.expert_in.2 B.omega.1 "
        "E.expert_out.2 D.mix.3 E.expert_in.3 C.center.0 E.expert_out.3 C.variance.0 B.omega.2 E.expert_in.4 "
        "C.normalise.0 E.expert_out.4 D.r_out.0 E.expert_in.5 E.expert_out.5 C.gate.0 B.omega.3 E.expert_in.6 "
        "C.soft.0 E.expert_out.6 C.top.0 E.expert_in.7 C.weights.0 B.r_out.0 E.expert_out.7 A.conv_load.0 "
        "E.residual.0 A.conv.0 E.center2.0 C.h2.0 A.conv_fold.0 E.variance2.0 C.h2.1 A.conv_out.0 E.normalise2.0 "
        "C.r_out.0 "
    ),
    "pool": (
        "D.variance.0 E.variance.0 D.normalise.0 B.variance.0 E.normalise.0 B.normalise.0 D.window_k.0 "
        "E.weights.0 C.variance.0 C.normalise.0 C.weights.0 A.conv.0 E.variance2.0 "
    ),
}


def schedule(name, active):
    for word in ORDER[name].split():
        s, step, k = word.split(".")
        if "ABCDE".index(s) in active:
            yield step, "ABCDE".index(s), int(k)


class Counts:

    def __init__(self, eng, it):
        self.eng, self.it, self.known = eng, it, {}

    def __call__(self, s, per=1, more=None):
        more = per if more is None else more
        if isinstance(self.it, int):
            return per * (self.it - s) + more
        key = (per, more - per * s)
        if key not in self.known:
            self.known[key] = self.eng.snap(self.it * per + (more - per * s))
        return self.known[key]

    def before(self, s, per=1):
        return self(s, per, 0)


def tower(nc, x, split_w, plain_w, exact_w, out):
    with ExitStack() as ctx:
        def sb(name, shape, dt=F32):
            return ctx.enter_context(nc.sbuf_tensor(name, shape, dt))

        def sem(name):
            return ctx.enter_context(nc.semaphore(name))

        h_all = sb("h_all", [128, B * F])
        split_in = h_all[:, 0:NSPLIT]
        exact_in = h_all[:, NSPLIT:NSPLIT + NEXACT]
        split_hi = sb("split_hi", [128, NSPLIT], F32R)
        split_lo = sb("split_lo", [128, NSPLIT], F32R)
        plain = sb("plain", [128, NPLAIN])
        exact = sb("exact", [128, NEXACT], F32R)
        neg_alpha = sb("neg_alpha", [128, 1])
        alpha_tau = sb("alpha_tau", [128, 1])
        minus_half = sb("minus_half", [128, G])
        half = sb("half", [128, G])
        eps_tile = sb("eps_tile", [128, G])

        def hi(name, a=0, n=None):
            at, w = SPLIT_AT[name]
            return split_hi[:, at + a:at + a + (n or w)]

        def lo(name, a=0, n=None):
            at, w = SPLIT_AT[name]
            return split_lo[:, at + a:at + a + (n or w)]

        def pl(name, a=0, n=None, rows=slice(0, 128)):
            at, w = PLAIN_AT[name]
            return plain[rows, at + a:at + a + (n or w)]

        def ex(name, a=0, n=None):
            at, w = EXACT_AT[name]
            return exact[:, at + a:at + a + (n or w)]

        tok = slice(0, L)
        x_in = sb("x_in", [128, G * CIN])
        x_sq = sb("x_sq", [128, G * CIN])
        x_hi = sb("x_hi", [128, G * LX], F32R)
        x_lo = sb("x_lo", [128, G * LX], F32R)
        sq_sum = sb("sq_sum", [128, G])
        energy = sb("energy", [128, G])
        norm = sb("norm", [128, G])
        gate_exp = sb("gate_exp", [128, G])
        gate_den = sb("gate_den", [128, G])
        gate_all = sb("gate_all", [128, G])
        gate_inv = sb("gate_inv", [128, G])
        gate_tok = sb("gate_tok", [128, G])
        conv_odd = x_sq[0:64, 0:N]
        conv_t = conv_odd
        LN = range(B_, E_ + 2)
        total = {s: sb(f"total{s}", [128, G]) for s in LN}
        centered = {s: sb(f"centered{s}", [128, GF]) for s in LN}
        var = {s: sb(f"var{s}", [128, G]) for s in LN}
        var_eps = {s: sb(f"var_eps{s}", [128, G]) for s in LN}
        rstd = {s: sb(f"rstd{s}", [128, G]) for s in LN}
        normed = {s: sb(f"normed{s}", [128, GF]) for s in LN}
        squares = normed
        parts = {s: sb(f"parts{s}", [128, G * 128], F32R) for s in range(B_, E_ + 1)}
        feats = {s: sb(f"feats{s}", [128, N], F32R) for s in range(B_, E_ + 1)}
        keys = [sb(f"keys{i}", [128, N]) for i in range(2)]
        queries = sb("queries", [128, G * NP0 * L])
        omega = sb("omega", [128, 2 * NP0 * L])
        zed = sb("zed", [128, NP0 * N])
        result = {B_: omega[:, 0:2 * L]}
        NE = {C_: E0, E_: E1}
        logit = {s: sb(f"logit{s}", [128, G * NE[s]]) for s in NE}
        logit2 = {s: sb(f"logit2{s}", [128, G * NE[s]]) for s in NE}
        equal = {s: sb(f"equal{s}", [128, G * NE[s]]) for s in NE}
        first = {s: sb(f"first{s}", [128, G * NE[s]]) for s in NE}
        second = {s: sb(f"second{s}", [128, G * NE[s]]) for s in NE}
        best = {s: sb(f"best{s}", [128, G]) for s in NE}
        next_best = {s: sb(f"next_best{s}", [128, G]) for s in NE}
        rank = {s: sb(f"rank{s}", [128, G]) for s in NE}
        gap = {s: sb(f"gap{s}", [128, G]) for s in NE}
        gap_exp = {s: sb(f"gap_exp{s}", [128, G]) for s in NE}
        w_first = {s: sb(f"w_first{s}", [128, G]) for s in NE}
        w_second = {s: sb(f"w_second{s}", [128, G]) for s in NE}
        weight = {s: sb(f"weight{s}", [128, G * NE[s]]) for s in NE}
        w_parts = {s: sb(f"w_parts{s}", [128, G * 2 * NE[s]], F32R) for s in NE}
        w_feats = {s: sb(f"w_feats{s}", [128, N], F32R) for s in NE}
        prob_in = sb("prob_in", [128, G * E0])
        prob_exp = sb("prob_exp", [128, G * E0])
        prob_sum = sb("prob_sum", [128, G])
        prob = sb("prob", [128, G * E0])
        hid1 = sb("hid1", [128, (E0 + 1) * N])
        hid2 = sb("hid2", [128, 3 * N])
        result[C_] = hid1[:, 0:2 * L]
        q_bd = sb("q_bd", [128, G * NW * WS])
        k_win = sb("k_win", [128, G * WS])
        k_head = sb("k_head", [128, G * NH1 * WS])
        v_bd = sb("v_bd", [128, G * 4 * 32])
        neg_max = sb("neg_max", [128, NH1])
        probs = sb("probs", [128, NH1 * WS])
        shifted = probs
        probs_t = sb("probs_t", [128, NH1 * WS])
        result[D_] = probs_t[:, 0:2 * L]
        inv_sum = sb("inv_sum", [128, 128])
        mixed = sb("mixed", [128, G * 128])
        hid_e = [sb(f"hid_e{i}", [128, N]) for i in range(4)]
        moe = hid_e[0]
        y_res = normed[E_ + 1]
        y_out = sb("y_out", [128, GF])

        bank = [ctx.enter_context(nc.psum_tensor(f"bank{i}", [128, 512], F32)) for i in range(8)]

        weights_in = sem("weights_in")
        exact_loaded = sem("exact_loaded")
        hi_made = sem("hi_made")
        weights_split = sem("weights_split")
        exact_made = sem("exact_made")
        setup_done = sem("setup_done")
        x_loaded = sem("x_loaded")
        x_turned = sem("x_turned")
        x_hi_made = sem("x_hi_made")
        x_lo_made = sem("x_lo_made")
        x_squared = sem("x_squared")
        sq_summed = sem("sq_summed")
        energy_sum = sem("energy_sum")
        energy_read = sem("energy_read")
        norm_made = sem("norm_made")
        gate_exp_made = sem("gate_exp_made")
        conv_done = sem("conv_done")
        conv_odd_made = sem("conv_odd_made")
        conv_folded = sem("conv_folded")
        conv_turned = sem("conv_turned")
        h_ready = {A_: sem("h_conv"), B_: sem("h_causal"), C_: sem("h_mlp"), D_: sem("h_window")}
        ln_centered = {s: sem(f"ln_centered{s}") for s in LN}
        ln_squared = {s: sem(f"ln_squared{s}") for s in LN}
        ln_var = {s: sem(f"ln_var{s}") for s in LN}
        ln_rstd = {s: sem(f"ln_rstd{s}") for s in LN}
        st = range(B_, E_ + 1)
        ln_normed = {s: sem(f"ln_normed{s}") for s in st}
        parts_hi = {s: sem(f"parts_hi{s}") for s in st}
        parts_lo = {s: sem(f"parts_lo{s}") for s in st}
        feats_psum = {s: sem(f"feats_psum{s}") for s in st}
        feats_made = {s: sem(f"feats_made{s}") for s in st}
        keys_psum = sem("keys_psum")
        keys_made = sem("keys_made")
        q_psum = sem("q_psum")
        q_made = sem("q_made")
        om_psum = [sem(f"om_psum{i}") for i in range(2)]
        om_masked = [sem(f"om_masked{i}") for i in range(2)]
        z_psum = sem("z_psum")
        z_made = sem("z_made")
        res_psum = {s: sem(f"res_psum{s}") for s in (B_, C_, D_)}
        res_made = {s: sem(f"res_made{s}") for s in (B_, C_, D_)}
        res_turned = {s: sem(f"res_turned{s}") for s in (B_, C_, D_)}
        lg_psum = {s: sem(f"lg_psum{s}") for s in NE}
        lg_read = {s: sem(f"lg_read{s}") for s in NE}
        gap_made = {s: sem(f"gap_made{s}") for s in NE}
        gap_exp_made = {s: sem(f"gap_exp_made{s}") for s in NE}
        weight_made = {s: sem(f"weight_made{s}") for s in NE}
        w_hi_made = {s: sem(f"w_hi_made{s}") for s in NE}
        w_lo_made = {s: sem(f"w_lo_made{s}") for s in NE}
        w_psum = {s: sem(f"w_psum{s}") for s in NE}
        w_feats_made = {s: sem(f"w_feats_made{s}") for s in NE}
        prob_shifted = sem("prob_shifted")
        prob_exp_made = sem("prob_exp_made")
        h1s_psum = sem("h1s_psum")
        h1s_made = sem("h1s_made")
        h1_psum = sem("h1_psum")
        h1_made = sem("h1_made")
        h2_psum = [sem("h2_psum0"), sem("h2_psum1"), sem("h2_psum_shared")]
        relu2_made = [sem("relu2_made0"), sem("relu2_made1")]
        h2_made = [sem("h2_made0"), sem("h2_made1"), sem("h2_made_shared")]
        wq_psum, wk_psum, wv_psum = sem("wq_psum"), sem("wk_psum"), sem("wv_psum")
        wq_made, wk_made, wv_made = sem("wq_made"), sem("wk_made"), sem("wv_made")
        k_masked = sem("k_masked")
        s_psum = sem("s_psum")
        s_shifted = sem("s_shifted")
        p_made = sem("p_made")
        pt_psum = sem("pt_psum")
        pt_made = sem("pt_made")
        u_psum = sem("u_psum")
        u_made = sem("u_made")
        e_psum = [sem(f"e_psum{i}") for i in range(4)]
        e_relu = [sem(f"e_relu{i}") for i in range(4)]
        e_share = [sem(f"e_share{i}") for i in range(4)]
        e_weighted = [sem(f"e_weighted{i}") for i in range(4)]
        e_summed = [sem(f"e_summed{i}") for i in range(2)]
        moe_psum = sem("moe_psum")
        moe_made = sem("moe_made")
        moe_turned = sem("moe_turned")
        out_made = sem("out_made")
        out_stored = sem("out_stored")

        def hg(it, s):
            return h_all[tok, bass.ds((it - s) * GF, GF)]

        def per_seq(ap):
            return ap.rearrange("p (b f) -> p b f", b=G)

        def over_f(ap, n=F):
            return ap.unsqueeze(2).to_broadcast([L, G, n])

        def over_b(ap, n):
            return ap.unsqueeze(1).to_broadcast([L, G, n])

        def run(eng, name, steps):
            def iteration(it, active):
                n = Counts(eng, it)
                for step, s, k in schedule(name, active):
                    if step in steps:
                        steps[step](n, it, s, k)

            for t in range(STAGES):
                iteration(t, range(0, t + 1))
            with eng.Fori(STAGES, NG) as it:
                iteration(it, range(STAGES))
            for t in range(NG, NG + STAGES - 1):
                iteration(t, range(t - NG + 1, STAGES))

        block = ctx.enter_context(nc.Block())

        @block.sync
        def _(sp):
            sp.dma_start(split_in[:], split_w).then_inc(weights_in, 16)
            sp.dma_start(plain[:], plain_w).then_inc(weights_in, 16)
            sp.dma_start(exact_in[:, 0:NEXACT], exact_w).then_inc(exact_loaded, 16)

            def load(n, it, s, k):
                sp.wait_ge(x_turned, n.before(A_))
                sp.wait_ge(x_squared, n.before(A_))
                sp.dma_start(x_in[0:LX, :].rearrange("t (b c) -> t b c", b=G),
                             x[bass.ds((it - A_) * G, G), :, :].rearrange("b t c -> t b c")).then_inc(x_loaded, 16)

            def store(n, it, s, k):
                sp.wait_ge(out_made, n(E_))
                sp.dma_start(out[bass.ds((it - E_) * G, G), :, :].rearrange("b t f -> t b f"),
                             per_seq(y_out[tok, :])).then_inc(out_stored, 16)

            for t in range(STAGES):
                load(Counts(sp, t), t, A_, 0)
            store(Counts(sp, STAGES - 1), STAGES - 1, E_, 0)
            with sp.Fori(STAGES, NG) as it:
                n = Counts(sp, it)
                load(n, it, A_, 0)
                store(n, it, E_, 0)
            for t in range(NG, NG + STAGES - 1):
                store(Counts(sp, t), t, E_, 0)
            sp.wait_ge(out_stored, 16 * NG)

        @block.tensor
        def _(pe):
            mm = nc.tensor.matmul
            pe.wait_ge(setup_done, 2)
            ident = pl("ident")

            def to_features(n, it, s, k):
                to = {B_: bank[0], C_: bank[2], D_: bank[2], E_: bank[4]}[s]
                if s == B_:
                    pe.wait_ge(conv_turned, n(B_))
                elif s == C_:
                    pe.wait_ge(h_ready[D_], n.before(C_))
                pe.wait_ge(parts_lo[s], n(s))
                for b in range(G):
                    last = nc.tensor.transpose(to[:, b * L:(b + 1) * L], parts[s][tok, b * 128:(b + 1) * 128].bitcast(F32),
                                               ident[tok, 0:L])
                last.then_inc(feats_psum[s], 1)

            def conv_load(n, it, s, k):
                pe.wait_ge(x_loaded, n(A_, 16))
                pe.wait_ge(h_ready[B_], n.before(A_))
                for b in range(G):
                    last = nc.tensor.transpose(bank[0][:, b * LX:(b + 1) * LX], x_in[0:LX, b * CIN:(b + 1) * CIN],
                                               ident[0:LX, 0:LX])
                last.then_inc(x_turned, 1)

            def conv(n, it, s, k):
                pe.wait_ge(x_lo_made, n(A_))
                pe.wait_ge(sq_summed, n(A_))
                mm(bank[0][tok, 0:G], pl("band", rows=slice(0, LX)), sq_sum[0:LX, :], start=True,
                   stop=True).then_inc(energy_sum, 1)
                xh = x_hi[:, :].rearrange("c (b t) -> c b t", b=G)
                xl = x_lo[:, :].rearrange("c (b t) -> c b t", b=G)
                for j in range(TP):
                    for i, (w, v) in enumerate(((hi, xh), (hi, xl), (lo, xh))):
                        last = mm(bank[1][:, 0:G * LC], w("conv", j * 128, 128), v[:, :, 2 * j:2 * j + LC] if 2 * j + LC <= LX
                                  else v[:, :, LX - LC:LX], start=(j == 0 and i == 0), stop=(j == TP - 1 and i == 2))
                last.then_inc(conv_done, 1)

            def conv_out(n, it, s, k):
                pe.wait_ge(conv_folded, n(A_))
                for b in range(G):
                    last = nc.tensor.transpose(bank[0][tok, b * 128:(b + 1) * 128], x_sq[:, b * L:(b + 1) * L], ident)
                last.then_inc(conv_turned, 1)

            def keys_step(n, it, s, k):
                pe.wait_ge(feats_made[B_], n(B_))
                mm(bank[1][:, 0:N], pl("fold"), feats[B_][:, :].bitcast(F32), start=True, stop=True).then_inc(keys_psum, 1)

            def query(n, it, s, p):
                if p == 1:
                    pe.wait_ge(keys_made, n(B_))
                elif p >= 2:
                    pe.wait_ge(q_made, n(B_, 4, p - 1))
                to = bank[p % 2][:, 0:N]
                mm(to, hi("q0", p * 128, 128), feats[B_][:, :], start=True, stop=False)
                mm(to, lo("q0", p * 128, 128), feats[B_][:, :], start=False, stop=True).then_inc(q_psum, 1)

            def omega_bank(b, par):
                return bank[(b + par) % 2]

            def omega_step(n, it, s, b):
                for par in range(2):
                    if b == 0 and par == 0:
                        pe.wait_ge(q_made, n(B_, 4))
                    if b > 0 and par == 0:
                        pe.wait_ge(om_masked[1], n(B_, 4, b))
                    if b > 0 and par == 1:
                        pe.wait_ge(z_made, n(B_, 4, b))
                    to = omega_bank(b, par)[tok, 0:NP0 * L]
                    mm(to, keys[par][:, b * L:(b + 1) * L], queries[:, b * NP0 * L:(b + 1) * NP0 * L], start=True,
                       stop=True).then_inc(om_psum[par], 1)

            def zed_step(n, it, s, b):
                pe.wait_ge(om_masked[0], n(B_, 4, b + 1))
                pe.wait_ge(om_masked[1], n(B_, 4, b + 1))
                for par in range(2):
                    last = mm(omega_bank(b, 0)[64 * par:64 * par + 64, 0:NP0 * L], normed[B_][tok, b * F:(b + 1) * F],
                              omega[tok, par * NP0 * L:(par + 1) * NP0 * L], start=True, stop=True)
                last.then_inc(z_psum, 1)

            def r_step(n, it, s, k):
                pe.wait_ge(z_made, n(B_, 4))
                for p in range(NP0):
                    for half_ in range(2):
                        last = mm(bank[0][64 * half_:64 * half_ + 64, 0:2 * L], pl("e0", p * F, F),
                                  zed[:, p * N + half_ * 2 * L:p * N + (half_ + 1) * 2 * L],
                                  start=(p == 0), stop=(p == NP0 - 1))
                last.then_inc(res_psum[B_], 1)

            def r_out(n, it, s, k):
                to = {B_: bank[1], C_: bank[2], D_: bank[3]}[s]
                pe.wait_ge(res_made[s], n(s))
                for j in range(2):
                    last = nc.tensor.transpose(to[tok, j * 128:(j + 1) * 128], result[s][:, j * L:(j + 1) * L], ident)
                last.then_inc(res_turned[s], 1)

            def gate(n, it, s, k):
                to = bank[3] if s == C_ else bank[5]
                pe.wait_ge(feats_made[s], n(s))
                for b in range(G):
                    last = mm(to[tok, b * NE[s]:(b + 1) * NE[s]], feats[s][:, b * L:(b + 1) * L].bitcast(F32),
                              pl("gwc" if s == C_ else "gwe"), start=True, stop=True)
                last.then_inc(lg_psum[s], 1)

            def weights(n, it, s, k):
                to = bank[3] if s == C_ else bank[6]
                m = 2 * NE[s]
                if s == C_:
                    pe.wait_ge(h1_made, n(C_, 4, 3))
                pe.wait_ge(w_lo_made[s], n(s))
                for b in range(G):
                    last = nc.tensor.transpose(to[0:m, b * L:(b + 1) * L], w_parts[s][tok, b * m:(b + 1) * m].bitcast(F32),
                                               ident[tok, 0:L])
                last.then_inc(w_psum[s], 1)

            def two_pass(to, name, at, v):
                mm(to, hi(name, at, 128), v, start=True, stop=False)
                return mm(to, lo(name, at, 128), v, start=False, stop=True)

            def h1_shared(n, it, s, k):
                two_pass(bank[2][:, 0:N], "w1c", E0 * 128, feats[C_][:, :]).then_inc(h1s_psum, 1)

            def h1(n, it, s, e):
                if e == 0:
                    pe.wait_ge(lg_read[C_], n(C_))
                elif e == 1:
                    pe.wait_ge(h1s_made, n(C_))
                else:
                    pe.wait_ge(h1_made, n(C_, 4, e - 1))
                two_pass(bank[3 - e % 2][:, 0:N], "w1c", e * 128, feats[C_][:, :]).then_inc(h1_psum, 1)

            def h2(n, it, s, p):
                if p == 0:
                    pe.wait_ge(h1_made, n(C_, 4))
                    pe.wait_ge(w_feats_made[C_], n(C_))
                else:
                    pe.wait_ge(relu2_made[0], n(C_))
                for i in range(2):
                    last = mm(bank[2][64 * i:64 * i + 64, 0:N], pl("w2c", (2 * p + i) * F, F),
                              hid1[:, (2 * p + i) * N:(2 * p + i + 1) * N], start=True, stop=True)
                if p == 1:
                    pe.wait_ge(h2_made[0], n(C_))
                mm(bank[3][:, 0:N], ex("sel_c", p * 128, 128), w_feats[C_][:, :], start=True,
                   stop=True).then_inc(h2_psum[p], 1)

            def h2_shared(n, it, s, k):
                pe.wait_ge(relu2_made[1], n(C_))
                mm(bank[2][:, 0:N], pl("w2s"), hid1[:, E0 * N:(E0 + 1) * N], start=True,
                   stop=True).then_inc(h2_psum[2], 1)

            def mlp_out(n, it, s, k):
                pe.wait_ge(h2_made[1], n(C_))
                pe.wait_ge(h2_made[2], n(C_))
                for i in range(4):
                    for half_ in range(2):
                        cols = slice(half_ * 2 * L, (half_ + 1) * 2 * L)
                        v = hid2[:, i * N:(i + 1) * N][:, cols] if i < 3 else w_feats[C_][:, cols].bitcast(F32)
                        w = pl("w3c", i * F, F) if i < 3 else pl("eb3")
                        last = mm(bank[3][64 * half_:64 * half_ + 64, 0:2 * L], w, v, start=(i == 0), stop=(i == 3))
                last.then_inc(res_psum[C_], 1)

            def window_q(n, it, s, k):
                pe.wait_ge(feats_made[D_], n(D_))
                two_pass(bank[3][:, 0:N], "wq", 0, feats[D_][:, :]).then_inc(wq_psum, 1)

            def window_k(n, it, s, k):
                two_pass(bank[2][:, 0:N], "wk", 0, feats[D_][:, :]).then_inc(wk_psum, 1)

            def window_v(n, it, s, k):
                pe.wait_ge(wq_made, n(D_))
                for b in range(G):
                    last = mm(bank[3][tok, b * 128:(b + 1) * 128], feats[D_][:, b * L:(b + 1) * L].bitcast(F32), pl("wv"),
                              start=True, stop=True)
                last.then_inc(wv_psum, 1)

            def score(n, it, s, b):
                if b == 0:
                    pe.wait_ge(k_masked, n(D_))
                else:
                    pe.wait_ge(s_shifted, n(D_, 4, b))
                mm(bank[2][:, :], q_bd[:, b * 128:(b + 1) * 128], k_head[:, b * 512:(b + 1) * 512], start=True, stop=False)
                mm(bank[2][:, :], ex("query"), ex("rel"), start=False, stop=True).then_inc(s_psum, 1)

            def flip(n, it, s, b):
                pe.wait_ge(p_made, n(D_, 4, b + 1))
                if b == 0:
                    pe.wait_ge(wv_made, n(D_))
                else:
                    pe.wait_ge(u_made, n(D_, 4, b))
                for p in range(4):
                    last = nc.tensor.transpose(bank[3][:, p * 128:(p + 1) * 128], probs[:, p * 128:(p + 1) * 128], ident)
                last.then_inc(pt_psum, 1)

            def mix(n, it, s, b):
                pe.wait_ge(pt_made, n(D_, 4, b + 1))
                for at, w in ((0, None), (128, pl("ones_bd"))):
                    for p in range(4):
                        v = v_bd[:, (b * 4 + p) * 32:(b * 4 + p + 1) * 32] if w is None else w
                        last = mm(bank[3][32 * p:32 * p + 32, at:at + 128], v, probs_t[:, p * 128:(p + 1) * 128],
                                  start=True, stop=True)
                last.then_inc(u_psum, 1)

            def project(n, it, s, k):
                pe.wait_ge(u_made, n(D_, 4))
                for half_ in range(2):
                    last = mm(bank[2][64 * half_:64 * half_ + 64, 0:2 * L], pl("wp"),
                              mixed[:, :].rearrange("p (b q) -> p b q", b=G)[:, 2 * half_:2 * half_ + 2, tok],
                              start=True, stop=True)
                last.then_inc(res_psum[D_], 1)

            def share(n, e):
                mm(bank[6][:, 0:N], ex("sel_e", e, 1).to_broadcast([128, 128]), w_feats[E_][:, :], start=True,
                   stop=True).then_inc(e_share[e % 4], 1)

            def first_layer(n, e):
                two_pass(bank[4 + e % 2][:, 0:N], "w1e", e * 128, feats[E_][:, :]).then_inc(e_psum[e % 4], 1)

            def second_layers(n, j):
                pe.wait_ge(e_weighted[(2 * j + 1) % 4], n(E_, 4, (2 * j + 1) // 4 + 1))
                for i in range(2):
                    last = mm(bank[7][64 * i:64 * i + 64, 0:N], pl("w2e", (2 * j + i) * F, F), hid_e[(2 * j + i) % 4][:, :],
                              start=(j == 0), stop=(j == E1 // 2 - 1 and i == 1))
                last.then_inc(e_summed[j % 2], 1)

            def expert_in(n, it, s, j):
                if j == 0:
                    pe.wait_ge(w_feats_made[E_], n(E_))
                    pe.wait_ge(moe_made, n.before(E_))
                    pe.wait_ge(lg_read[E_], n(E_))
                else:
                    pe.wait_ge(e_weighted[(2 * j - 1) % 4], n(E_, 4, (2 * j - 1) // 4 + 1))
                share(n, 2 * j)
                first_layer(n, 2 * j)
                first_layer(n, 2 * j + 1)

            def expert_out(n, it, s, j):
                pe.wait_ge(e_weighted[(2 * j) % 4], n(E_, 4, (2 * j) // 4 + 1))
                share(n, 2 * j + 1)
                if j:
                    second_layers(n, j - 1)

            def expert_last(n, it, s, k):
                second_layers(n, E1 // 2 - 1)
                mm(bank[7][0:64, 0:N], pl("b2e"), w_feats[E_][:, :].bitcast(F32), start=False, stop=True)\
                    .then_inc(moe_psum, 1)

            def residual(n, it, s, k):
                pe.wait_ge(moe_made, n(E_))
                for b in range(G):
                    last = nc.tensor.transpose(bank[4][tok, b * 128:(b + 1) * 128], moe[:, b * L:(b + 1) * L], ident)
                last.then_inc(moe_turned, 1)

            run(pe, "pe", {"to_features": to_features, "conv_load": conv_load, "conv": conv, "conv_out": conv_out,
                           "keys": keys_step, "query": query, "omega": omega_step, "zed": zed_step, "r": r_step, "r_out": r_out,
                           "gate": gate, "weights": weights, "h1_shared": h1_shared, "h1": h1, "h2": h2,
                           "h2_shared": h2_shared, "mlp_out": mlp_out, "window_q": window_q, "window_k": window_k,
                           "window_v": window_v, "score": score, "flip": flip, "mix": mix, "project": project,
                           "expert_in": expert_in, "expert_out": expert_out, "expert_last": expert_last,
                           "residual": residual})

        @block.scalar
        def _(act):
            fn = nc.scalar.activation
            act.wait_ge(weights_in, 32)
            at = SPLIT_AT["wq"][0]
            fn(split_in[:, at:at + 128], split_in[:, at:at + 128], ACT.Copy, scale=float(HD) ** -0.5)
            nc.scalar.drain()
            fn(split_hi[:, :], split_in[:, :], ACT.Copy).then_inc(hi_made, 1)
            act.wait_ge(exact_loaded, 16)
            fn(exact[:, :], exact_in[:, 0:NEXACT], ACT.Copy).then_inc(exact_made, 1)
            act.wait_ge(exact_made, 1)
            act.wait_ge(setup_done, 2)

            def center(n, it, s, k):
                act.wait_ge(ln_centered[s], n(min(s, E_)))
                if s <= E_:
                    act.wait_ge(parts_lo[s], n.before(s))
                if s == B_:
                    act.wait_ge(z_psum, n(B_, 4, 0))
                if s == E_:
                    act.wait_ge(ln_centered[s + 1], n.before(E_))
                fn(squares[s][tok, :], centered[s][tok, :], ACT.Square,
                   scale=float(F) ** -0.5).then_inc(ln_squared[s], 1)

            def normalise(n, it, s, k):
                act.wait_ge(ln_normed[s], n(s))
                act.wait_ge(feats_psum[s], n.before(s))
                fn(parts[s][tok, :].rearrange("p (b c f) -> p b c f", b=G, c=2)[:, :, 0, :], per_seq(normed[s][tok, :]),
                   ACT.Copy).then_inc(parts_hi[s], 1)

            def to_features(n, it, s, k):
                frm = {B_: bank[0], C_: bank[2], D_: bank[2], E_: bank[4]}[s]
                act.wait_ge(feats_psum[s], n(s))
                fn(feats[s][:, :], frm[:, 0:N], ACT.Copy).then_inc(feats_made[s], 1)

            def conv_load(n, it, s, k):
                act.wait_ge(x_loaded, n(A_, 16))
                act.wait_ge(conv_turned, n.before(A_))
                fn(x_sq[0:LX, :], x_in[0:LX, :], ACT.Square).then_inc(x_squared, 1)
                act.wait_ge(x_turned, n(A_))
                act.wait_ge(conv_done, n.before(A_))
                fn(x_hi[:, :], bank[0][:, 0:G * LX], ACT.Copy).then_inc(x_hi_made, 1)

            def conv_fold(n, it, s, k):
                act.wait_ge(norm_made, n(A_))
                fn(gate_exp[tok, :], norm[tok, :], ACT.Exp, scale=neg_alpha[tok, :], bias=alpha_tau[tok, :])\
                    .then_inc(gate_exp_made, 1)
                act.wait_ge(sq_summed, n(A_))
                act.wait_ge(conv_done, n(A_))
                fn(conv_odd[:, :].rearrange("f (b t) -> f b t", b=G),
                   bank[1][64:128, 0:G * LC].rearrange("f (b t) -> f b t", b=G)[:, :, 1:LC], ACT.Copy)\
                    .then_inc(conv_odd_made, 1)

            def keys_step(n, it, s, k):
                act.wait_ge(keys_psum, n(B_))
                act.wait_ge(om_psum[1], n(B_, 4, 0))
                fn(keys[0][0:64, :], bank[1][0:64, 0:N], ACT.Copy)
                fn(keys[1][64:128, :], bank[1][64:128, 0:N], ACT.Copy).then_inc(keys_made, 1)

            def query(n, it, s, p):
                act.wait_ge(q_psum, n(B_, 4, p + 1))
                fn(queries[:, :].rearrange("j (b p t) -> j b p t", b=G, p=NP0)[:, :, p, :],
                   bank[p % 2][:, 0:N].rearrange("j (b t) -> j b t", b=G), ACT.Copy).then_inc(q_made, 1)

            def zed_step(n, it, s, b):
                act.wait_ge(z_psum, n(B_, 4, b + 1))
                if b == 0:
                    act.wait_ge(res_psum[B_], n.before(B_))
                fn(zed[:, :].rearrange("j (p b t) -> j p b t", p=NP0, b=G)[:, :, b, :],
                   bank[b % 2][:, 0:NP0 * L].rearrange("j (p t) -> j p t", p=NP0), ACT.Copy).then_inc(z_made, 1)

            def take_result(n, s, frm, bias):
                act.wait_ge(res_psum[s], n(s))
                act.wait_ge(res_turned[s], n.before(s))
                if bias is None:
                    fn(result[s][:, :], frm[:, 0:2 * L], ACT.Copy).then_inc(res_made[s], 1)
                else:
                    fn(result[s][:, :], frm[:, 0:2 * L], ACT.Identity, bias=bias).then_inc(res_made[s], 1)

            def r_step(n, it, s, k):
                take_result(n, B_, bank[0], None)

            def mlp_out(n, it, s, k):
                take_result(n, C_, bank[3], pl("b3c"))

            def project(n, it, s, k):
                take_result(n, D_, bank[2], pl("bp"))

            def soft(n, it, s, k):
                act.wait_ge(prob_shifted, n(C_))
                fn(prob_exp[tok, :], prob_in[tok, :], ACT.Exp).then_inc(prob_exp_made, 1)

            def top(n, it, s, k):
                act.wait_ge(gap_made[s], n(s))
                fn(gap_exp[s][tok, :], gap[s][tok, :], ACT.Exp).then_inc(gap_exp_made[s], 1)

            def weights(n, it, s, k):
                act.wait_ge(weight_made[s], n(s))
                act.wait_ge(w_psum[s], n.before(s))
                fn(w_parts[s][tok, :].rearrange("p (b c e) -> p b c e", b=G, c=2)[:, :, 0, :],
                   weight[s][tok, :].rearrange("p (b e) -> p b e", b=G), ACT.Copy).then_inc(w_hi_made[s], 1)
                act.wait_ge(w_psum[s], n(s))
                frm = bank[3] if s == C_ else bank[6]
                fn(w_feats[s][0:2 * NE[s], :], frm[0:2 * NE[s], 0:N], ACT.Copy).then_inc(w_feats_made[s], 1)

            def h1_shared(n, it, s, k):
                act.wait_ge(h1s_psum, n(C_))
                fn(hid1[:, E0 * N:(E0 + 1) * N], bank[2][:, 0:N], ACT.Relu, bias=pl("b1c", E0, 1)).then_inc(h1s_made, 1)

            def h1(n, it, s, e):
                act.wait_ge(h1_psum, n(C_, 4, e + 1))
                if e == 0:
                    act.wait_ge(res_turned[C_], n.before(C_))
                fn(hid1[:, e * N:(e + 1) * N], bank[3 - e % 2][:, 0:N], ACT.Relu, bias=pl("b1c", e, 1)).then_inc(h1_made, 1)

            def h2(n, it, s, p):
                act.wait_ge(h2_psum[p], n(C_))
                if p == 0:
                    act.wait_ge(res_psum[C_], n.before(C_))
                fn(hid2[:, p * N:(p + 1) * N], bank[2][:, 0:N], ACT.Relu, bias=pl("b2c", p, 1)).then_inc(relu2_made[p], 1)

            def h2_shared(n, it, s, k):
                act.wait_ge(h2_psum[2], n(C_))
                fn(hid2[:, 2 * N:3 * N], bank[2][:, 0:N], ACT.Relu, bias=pl("b2c", 2, 1)).then_inc(h2_made[2], 1)

            def to_windows(dst, frm):
                v = frm[:, 0:N].rearrange("f (b t) -> f b t", b=G)
                fn(dst[0], v[0:64, :, 0:WS], ACT.Copy)
                return fn(dst[1], v[64:128, :, WS:L], ACT.Copy)

            def window_q(n, it, s, k):
                act.wait_ge(wq_psum, n(D_))
                v = q_bd[:, :].rearrange("f (b q) -> f b q", b=G)
                act.wait_ge(s_psum, n(D_, 4, 0))
                to_windows((v[0:64, :, 0:WS], v[64:128, :, WS:L]), bank[3]).then_inc(wq_made, 1)

            def window_k(n, it, s, k):
                act.wait_ge(wk_psum, n(D_))
                act.wait_ge(k_masked, n.before(D_))
                v = k_win[:, :].rearrange("f (b k) -> f b k", b=G)
                to_windows((v[0:64, :, 0:WS], v[64:128, :, 0:W1N]), bank[2]).then_inc(wk_made, 1)

            def window_v(n, it, s, k):
                act.wait_ge(wv_psum, n(D_))
                act.wait_ge(u_psum, n(D_, 4, 0))
                for w, rows in ((0, WS), (1, W1N)):
                    for h in range(2):
                        last = fn(v_bd[64 * h:64 * h + rows, :].rearrange("k (b x c) -> k b x c", b=G, c=32)
                                  [:, :, :, 16 * w + 8 * h:16 * w + 8 * h + 8],
                                  bank[3][64 * w:64 * w + rows, :].rearrange("k (b x c) -> k b x c", b=G, c=16)
                                  [:, :, 0:4, 8 * h:8 * h + 8], ACT.Copy)
                last.then_inc(wv_made, 1)

            def score(n, it, s, b):
                act.wait_ge(s_shifted, n(D_, 4, b + 1))
                fn(probs[:, :], shifted[:, :], ACT.Exp).then_inc(p_made, 1)

            def flip(n, it, s, b):
                act.wait_ge(pt_psum, n(D_, 4, b + 1))
                act.wait_ge(u_psum, n(D_, 4, b))
                if b == 0:
                    act.wait_ge(res_turned[D_], n.before(D_))
                fn(probs_t[:, :], bank[3][:, :], ACT.Copy).then_inc(pt_made, 1)

            def relu(n, e):
                act.wait_ge(e_psum[e % 4], n(E_, 4, e // 4 + 1))
                if e >= 4:
                    act.wait_ge(e_summed[(e // 2) % 2], n(E_, 4, (e - 4) // 4 + 1))
                else:
                    act.wait_ge(moe_turned, n.before(E_))
                fn(hid_e[e % 4][:, :], bank[4 + e % 2][:, 0:N], ACT.Relu, bias=pl("b1e", e, 1)).then_inc(e_relu[e % 4], 1)

            def expert_in(n, it, s, j):
                relu(n, 2 * j)
                relu(n, 2 * j + 1)

            def expert_last(n, it, s, k):
                act.wait_ge(moe_psum, n(E_))
                act.wait_ge(moe_turned, n.before(E_))
                fn(moe[:, :], bank[7][:, 0:N], ACT.Copy).then_inc(moe_made, 1)

            def center2(n, it, s, k):
                center(n, it, E_ + 1, k)

            run(act, "act", {"center": center, "normalise": normalise, "to_features": to_features,
                             "conv_load": conv_load, "conv_fold": conv_fold, "keys": keys_step, "query": query, "zed": zed_step,
                             "r": r_step, "mlp_out": mlp_out, "project": project, "soft": soft, "top": top,
                             "weights": weights, "h1_shared": h1_shared, "h1": h1, "h2": h2, "h2_shared": h2_shared,
                             "window_q": window_q, "window_k": window_k, "window_v": window_v, "score": score,
                             "flip": flip, "expert_in": expert_in, "expert_last": expert_last, "center2": center2})

        @block.vector
        def _(dve):
            v = nc.vector
            settle = nc.vector.drain

            dve.wait_ge(weights_in, 32)
            v.tensor_scalar(neg_alpha[:, :], pl("alpha"), -1.0, None, ALU.mult)
            v.tensor_tensor(alpha_tau[:, :], pl("alpha"), pl("tau"), ALU.mult)
            dve.wait_ge(hi_made, 1)
            v.tensor_tensor(split_lo[:, :], split_in[:, :], split_hi[:, :].bitcast(F32), ALU.subtract)\
                .then_inc(weights_split, 1)
            at, w = EXACT_AT["rel"]
            dve.wait_ge(exact_made, 1)
            v.tensor_tensor(exact[64:128, at:at + w], exact_in[64:128, at:at + w],
                            exact[64:128, at:at + w].bitcast(F32), ALU.subtract).then_inc(setup_done, 1)

            def center_of(n, s, src):
                v.tensor_reduce(total[s][tok, :], src, axis=AX, op=ALU.add)
                settle()
                v.scalar_tensor_tensor(out=per_seq(centered[s][tok, :]), in0=over_f(total[s][tok, :]), scalar=-1.0 / F,
                                       in1=src, op0=ALU.mult, op1=ALU.add).then_inc(ln_centered[s], 1)

            def center(n, it, s, k):
                dve.wait_ge(h_ready[s - 1], n(s))
                v.nop()
                center_of(n, s, per_seq(hg(it, s)))

            def variance(n, it, s, k):
                dve.wait_ge(ln_squared[s], n(min(s, E_)))
                v.tensor_reduce(var[s][tok, :], per_seq(squares[s][tok, :]), axis=AX, op=ALU.add).then_inc(ln_var[s], 1)

            def normalise(n, it, s, k):
                dve.wait_ge(ln_rstd[s], n(s))
                dve.wait_ge(parts_lo[s], n.before(s))
                v.tensor_tensor(per_seq(normed[s][tok, :]), per_seq(centered[s][tok, :]), over_f(rstd[s][tok, :]),
                                ALU.mult).then_inc(ln_normed[s], 1)

            def conv_load(n, it, s, k):
                dve.wait_ge(x_squared, n(A_))
                v.tensor_reduce(sq_sum[0:LX, :], x_sq[0:LX, :].rearrange("t (b c) -> t b c", b=G), axis=AX, op=ALU.add)\
                    .then_inc(sq_summed, 1)
                dve.wait_ge(x_hi_made, n(A_))
                v.tensor_tensor(x_lo[:, :], bank[0][:, 0:G * LX], x_hi[:, :].bitcast(F32), ALU.subtract)\
                    .then_inc(x_lo_made, 1)

            def conv(n, it, s, k):
                dve.wait_ge(energy_sum, n(A_))
                v.tensor_scalar(energy[tok, :], bank[0][tok, 0:G], EPS, None, ALU.add).then_inc(energy_read, 1)

            def conv_fold(n, it, s, k):
                dve.wait_ge(gate_exp_made, n(A_))
                v.tensor_scalar(gate_den[tok, :], norm[tok, :], EPS, None, ALU.add)
                settle()
                v.scalar_tensor_tensor(out=gate_all[tok, :], in0=gate_exp[tok, :], scalar=1.0, in1=gate_den[tok, :],
                                       op0=ALU.add, op1=ALU.mult)
                settle()
                v.reciprocal(gate_inv[tok, :], gate_all[tok, :])
                settle()
                v.tensor_scalar(gate_tok[tok, :], gate_inv[tok, :], pl("scale", rows=tok), None, ALU.mult)
                dve.wait_ge(conv_odd_made, n(A_))
                v.tensor_tensor(conv_t[:, :].rearrange("f (b t) -> f b t", b=G),
                                bank[1][0:64, 0:G * LC].rearrange("f (b t) -> f b t", b=G)[:, :, tok],
                                conv_odd[:, :].rearrange("f (b t) -> f b t", b=G), ALU.add).then_inc(conv_folded, 1)

            def conv_out(n, it, s, k):
                dve.wait_ge(conv_turned, n(A_))
                v.tensor_tensor(per_seq(hg(it, A_)), bank[0][tok, :].rearrange("p (b f) -> p b f", b=G)[:, :, 0:F], over_f(gate_tok[tok, :]), ALU.mult)
                settle()
                v.tensor_tensor(per_seq(hg(it, A_)), per_seq(hg(it, A_)), over_b(pl("bias_conv", rows=tok), F),
                                ALU.add).then_inc(h_ready[A_], 1)

            def omega_step(n, it, s, b):
                dve.wait_ge(z_psum, n(B_, 4, b))
                if b == 0:
                    dve.wait_ge(res_turned[B_], n.before(B_))
                for par in range(2):
                    dve.wait_ge(om_psum[par], n(B_, 4, b + 1))
                    by_pair = lambda ap: ap.rearrange("u (p t) -> u p t", p=NP0)
                    v.tensor_tensor(by_pair(omega[tok, par * NP0 * L:(par + 1) * NP0 * L]),
                                    by_pair(bank[(b + par) % 2][tok, 0:NP0 * L]),
                                    pl("causal", rows=tok).unsqueeze(1).to_broadcast([L, NP0, L]), ALU.mult)\
                        .then_inc(om_masked[par], 1)

            def r_out(n, it, s, k):
                frm = {B_: bank[1], C_: bank[2], D_: bank[3]}[s]
                dve.wait_ge(res_turned[s], n(s))
                cut = lambda ap: ap.rearrange("p (h j f) -> p j h f", h=2, j=2)
                v.tensor_tensor(cut(hg(it, s)), frm[tok, 0:GF].rearrange("p (j h f) -> p j h f", h=2, j=2), cut(hg(it, s)),
                                ALU.add).then_inc(h_ready[s], 1)

            def seqs(ap):
                return ap.rearrange("p (b e) -> p b e", b=G)

            def gate(n, it, s, k):
                e = NE[s]
                frm = bank[3] if s == C_ else bank[5]
                dve.wait_ge(lg_psum[s], n(s))
                v.tensor_tensor(seqs(logit[s][tok, :]), seqs(frm[tok, 0:G * e]),
                                over_b(pl("gbc" if s == C_ else "gbe", rows=tok), e), ALU.add).then_inc(lg_read[s], 1)
                settle()
                if s == C_:
                    v.tensor_reduce(best[s][tok, :], seqs(logit[s][tok, :]), axis=AX, op=ALU.max, negate=True)
                    settle()
                    v.tensor_tensor(seqs(prob_in[tok, :]), seqs(logit[s][tok, :]), over_f(best[s][tok, :], e), ALU.add)\
                        .then_inc(prob_shifted, 1)

            def soft(n, it, s, k):
                dve.wait_ge(prob_exp_made, n(C_))
                v.tensor_reduce(prob_sum[tok, :], seqs(prob_exp[tok, :]), axis=AX, op=ALU.add)
                settle()
                v.reciprocal(rank[C_][tok, :], prob_sum[tok, :])
                settle()
                v.tensor_tensor(seqs(prob[tok, :]), seqs(prob_exp[tok, :]), over_f(rank[C_][tok, :], E0), ALU.mult)
                settle()

            def pick(s, frm, value, chosen):
                e = NE[s]
                v.tensor_reduce(value[tok, :], frm, axis=AX, op=ALU.max)
                settle()
                v.tensor_tensor(seqs(equal[s][tok, :]), frm, over_f(value[tok, :], e), ALU.is_equal)
                settle()
                v.tensor_tensor(seqs(equal[s][tok, :]), seqs(equal[s][tok, :]),
                                over_b(pl("rank_c" if s == C_ else "rank_e", rows=tok), e), ALU.mult)
                settle()
                v.tensor_reduce(rank[s][tok, :], seqs(equal[s][tok, :]), axis=AX, op=ALU.max)
                settle()
                v.tensor_tensor(seqs(chosen[tok, :]), seqs(equal[s][tok, :]), over_f(rank[s][tok, :], e), ALU.is_equal)
                settle()

            def top(n, it, s, k):
                src = prob if s == C_ else logit[s]
                pick(s, seqs(src[tok, :]), best[s], first[s])
                v.scalar_tensor_tensor(out=logit2[s][tok, :], in0=first[s][tok, :], scalar=-BIG, in1=src[tok, :],
                                       op0=ALU.mult, op1=ALU.add)
                settle()
                pick(s, seqs(logit2[s][tok, :]), next_best[s], second[s])
                v.tensor_tensor(gap[s][tok, :], next_best[s][tok, :], best[s][tok, :], ALU.subtract).then_inc(gap_made[s], 1)

            def weights(n, it, s, k):
                e = NE[s]
                dve.wait_ge(gap_exp_made[s], n(s))
                v.tensor_scalar(rank[s][tok, :], gap_exp[s][tok, :], 1.0, None, ALU.add)
                settle()
                v.reciprocal(w_first[s][tok, :], rank[s][tok, :])
                settle()
                v.tensor_tensor(w_second[s][tok, :], gap_exp[s][tok, :], w_first[s][tok, :], ALU.mult)
                v.tensor_tensor(seqs(first[s][tok, :]), seqs(first[s][tok, :]), over_f(w_first[s][tok, :], e), ALU.mult)
                settle()
                v.tensor_tensor(seqs(second[s][tok, :]), seqs(second[s][tok, :]), over_f(w_second[s][tok, :], e), ALU.mult)
                settle()
                v.tensor_tensor(weight[s][tok, :], first[s][tok, :], second[s][tok, :], ALU.add).then_inc(weight_made[s], 1)

            def h2(n, it, s, p):
                dve.wait_ge(relu2_made[p], n(C_))
                v.tensor_tensor(hid2[:, p * N:(p + 1) * N], hid2[:, p * N:(p + 1) * N], bank[3][:, 0:N], ALU.mult).then_inc(h2_made[p], 1)

            def score(n, it, s, b):
                dve.wait_ge(s_psum, n(D_, 4, b + 1))
                by_head = bank[2][:, :].rearrange("q (h k) -> q h k", h=NH1)
                v.tensor_reduce(neg_max[:, :], by_head, axis=AX, op=ALU.max, negate=True)
                settle()
                dve.wait_ge(pt_psum, n(D_, 4, b))
                v.tensor_tensor(shifted[:, :].rearrange("q (h k) -> q h k", h=NH1), by_head,
                                neg_max[:, :].unsqueeze(2).to_broadcast([128, NH1, WS]), ALU.add).then_inc(s_shifted, 1)

            def mix(n, it, s, b):
                dve.wait_ge(u_psum, n(D_, 4, b + 1))
                v.reciprocal(inv_sum[:, :], bank[3][:, 128:256])
                settle()
                if b == 0:
                    dve.wait_ge(res_psum[D_], n.before(D_))
                for w in range(NW):
                    last = v.scalar_tensor_tensor(out=mixed[:, b * 128 + w * WS:b * 128 + (w + 1) * WS],
                                                  in0=bank[3][:, w * WS:(w + 1) * WS], scalar=pl("window", w, 1),
                                                  in1=inv_sum[:, w * WS:(w + 1) * WS], op0=ALU.mult, op1=ALU.mult)
                last.then_inc(u_made, 1)

            def weigh(n, e):
                dve.wait_ge(e_relu[e % 4], n(E_, 4, e // 4 + 1))
                dve.wait_ge(e_share[e % 4], n(E_, 4, e // 4 + 1))
                v.tensor_tensor(hid_e[e % 4][:, :], hid_e[e % 4][:, :], bank[6][:, 0:N], ALU.mult)\
                    .then_inc(e_weighted[e % 4], 1)

            def expert_in(n, it, s, j):
                weigh(n, 2 * j)

            def expert_out(n, it, s, j):
                weigh(n, 2 * j + 1)

            def residual(n, it, s, k):
                dve.wait_ge(moe_turned, n(E_))
                halves = bank[4][tok, :].rearrange("p (b c f) -> p b c f", b=G, c=2)
                v.tensor_tensor(per_seq(y_res[tok, :]), halves[:, :, 0, :], per_seq(normed[E_][tok, :]), ALU.add)
                settle()
                v.tensor_tensor(per_seq(y_res[tok, :]), halves[:, :, 1, :], per_seq(y_res[tok, :]), ALU.add)
                settle()

            def center2(n, it, s, k):
                center_of(n, E_ + 1, per_seq(y_res[tok, :]))

            def variance2(n, it, s, k):
                variance(n, it, E_ + 1, k)

            def normalise2(n, it, s, k):
                y = E_ + 1
                dve.wait_ge(ln_rstd[y], n(E_))
                v.tensor_tensor(per_seq(normed[y][tok, :]), per_seq(centered[y][tok, :]), over_f(rstd[y][tok, :]), ALU.mult)
                settle()
                v.tensor_tensor(per_seq(normed[y][tok, :]), per_seq(normed[y][tok, :]), over_b(pl("gamma", rows=tok), F), ALU.mult)
                settle()
                v.tensor_tensor(per_seq(normed[y][tok, :]), per_seq(normed[y][tok, :]), over_b(pl("beta", rows=tok), F), ALU.add)
                settle()
                dve.wait_ge(out_stored, n(E_, 16, 0))
                v.nop()
                v.tensor_tensor(y_out[tok, :], normed[y][tok, :], hg(it, E_), ALU.add).then_inc(out_made, 1)

            run(dve, "dve", {"center": center, "variance": variance, "normalise": normalise, "conv_load": conv_load,
                             "conv": conv, "conv_fold": conv_fold, "conv_out": conv_out,
                             "omega": omega_step, "r_out": r_out, "gate": gate, "soft": soft, "top": top,
                             "weights": weights, "h2": h2, "score": score, "mix": mix,
                             "expert_in": expert_in, "expert_out": expert_out, "residual": residual,
                             "center2": center2, "variance2": variance2, "normalise2": normalise2})

        @block.gpsimd
        def _(pool):
            g = nc.gpsimd
            for t in (x_sq, keys[0], keys[1], q_bd, k_win, v_bd, w_feats[C_], w_feats[E_]):
                g.memset(t[:, :].bitcast(F32) if t.dtype == F32R else t[:, :], 0.0)
            g.memset(minus_half[:, :], -0.5)
            g.memset(half[:, :], 0.5)
            g.memset(eps_tile[:, :], EPS)
            g.drain().then_inc(setup_done, 1)

            def variance(n, it, s, k):
                pool.wait_ge(ln_var[s], n(min(s, E_)))
                g.tensor_tensor(var_eps[s][tok, :], var[s][tok, :], eps_tile[tok, :], ALU.add)
                g.drain()
                g.tensor_tensor(rstd[s][tok, :], var_eps[s][tok, :], minus_half[tok, :], ALU.pow).then_inc(ln_rstd[s], 1)

            def normalise(n, it, s, k):
                pool.wait_ge(parts_hi[s], n(s))
                p = parts[s][tok, :].rearrange("p (b c f) -> p b c f", b=G, c=2)
                g.tensor_tensor(p[:, :, 1, :], per_seq(normed[s][tok, :]), p[:, :, 0, :].bitcast(F32), ALU.subtract)\
                    .then_inc(parts_lo[s], 1)

            def conv(n, it, s, k):
                pool.wait_ge(energy_read, n(A_))
                g.tensor_tensor(norm[tok, :], energy[tok, :], half[tok, :], ALU.pow).then_inc(norm_made, 1)

            def weights(n, it, s, k):
                pool.wait_ge(w_hi_made[s], n(s))
                p = w_parts[s][tok, :].rearrange("p (b c e) -> p b c e", b=G, c=2)
                g.tensor_tensor(p[:, :, 1, :], weight[s][tok, :].rearrange("p (b e) -> p b e", b=G),
                                p[:, :, 0, :].bitcast(F32), ALU.subtract).then_inc(w_lo_made[s], 1)

            def window_k(n, it, s, k):
                pool.wait_ge(wk_made, n(D_))
                pool.wait_ge(s_psum, n(D_, 4, 0))
                for b in range(G):
                    last = g.tensor_tensor(k_head[:, b * 512:(b + 1) * 512].rearrange("f (h k) -> f h k", h=NH1),
                                           k_win[:, b * WS:(b + 1) * WS].unsqueeze(1).to_broadcast([128, NH1, WS]),
                                           pl("head").unsqueeze(2).to_broadcast([128, NH1, WS]), ALU.mult)
                last.then_inc(k_masked, 1)

            def variance2(n, it, s, k):
                variance(n, it, E_ + 1, k)

            run(pool, "pool", {"variance": variance, "normalise": normalise, "conv": conv, "weights": weights,
                               "window_k": window_k, "variance2": variance2})


def _stack(w):
    return np.concatenate([w, w], axis=0)


def _layout(i):
    f = np.float32
    s = np.zeros((128, NSPLIT), f)
    p = np.zeros((128, NPLAIN), f)
    e = np.zeros((128, NEXACT), f)

    def put(to, at, name, a, col=0, row=0):
        a = np.asarray(a, f)
        assert col + a.shape[1] <= at[name][1]
        c = at[name][0] + col
        to[row:row + a.shape[0], c:c + a.shape[1]] = a

    k = i["L0_tok_kernel"]
    for t in range(TAPS):
        put(s, SPLIT_AT, "conv", k[t], (t // 2) * 128 + (64 if t % 2 or t == TAPS - 1 else 0))
    for h in range(NH0):
        q = i["L0_attn_Q"][h]
        put(s, SPLIT_AT, "q0", _stack(q), h * F)
        put(p, PLAIN_AT, "e0", i["L0_attn_E"][h].T, (h // 2) * F, 64 * (h % 2))
    for x in range(E0):
        put(s, SPLIT_AT, "w1c", _stack(i["L0_ffn_eW1"][x]), x * 128)
        put(p, PLAIN_AT, "w2c", i["L0_ffn_eW2"][x], x * F)
        put(p, PLAIN_AT, "w3c", i["L0_ffn_eW3"][x], (x // 2) * F, 64 * (x % 2))
        put(p, PLAIN_AT, "b1c", i["L0_ffn_eb1"][x][:, None], x)
        put(p, PLAIN_AT, "b2c", i["L0_ffn_eb2"][x][:, None], x // 2, 64 * (x % 2))
        for part in range(2):
            e[part * E0 + x, EXACT_AT["sel_c"][0] + x * F:EXACT_AT["sel_c"][0] + (x + 1) * F] = 1
    put(s, SPLIT_AT, "w1c", _stack(i["L0_ffn_sW1"]), E0 * 128)
    put(p, PLAIN_AT, "b1c", i["L0_ffn_sb1"][:, None], E0)
    put(p, PLAIN_AT, "w2s", i["L0_ffn_sW2"])
    put(p, PLAIN_AT, "b2c", i["L0_ffn_sb2"][:, None], 2)
    put(p, PLAIN_AT, "w3c", i["L0_ffn_sW3"], 2 * F)
    put(p, PLAIN_AT, "b3c", np.tile(i["L0_ffn_sb3"], 2)[:, None])
    put(p, PLAIN_AT, "eb3", _stack(i["L0_ffn_eb3"]))
    put(p, PLAIN_AT, "gwc", _stack(i["L0_ffn_gW"]))
    qkv = i["L1_attn_w_qkv"]
    put(s, SPLIT_AT, "wq", _stack(np.tile(qkv[0:64].T, (1, 2))))
    put(s, SPLIT_AT, "wk", _stack(np.tile(qkv[64:128].T, (1, 2))))
    put(p, PLAIN_AT, "wv", _stack(np.tile(qkv[128:192].T, (1, 2))))
    put(p, PLAIN_AT, "fold", np.tile(np.eye(64), (2, 2)))
    wp = i["L1_attn_w_proj"].T.reshape(4, 1, 2, HD, F)
    put(p, PLAIN_AT, "wp", np.tile(wp, (1, 2, 1, 1, 1)).reshape(128, F))
    put(p, PLAIN_AT, "bp", np.tile(i["L1_attn_b_proj"], 2)[:, None])
    pos = np.arange(WS)
    rel = i["L1_attn_rel_bias"][pos[None, :] - pos[:, None] + WS - 1]
    put(e, EXACT_AT, "rel", _stack(np.tile(rel, (1, NH1))))
    put(e, EXACT_AT, "query", np.tile(np.eye(WS), (2, 2)))
    for x in range(E1):
        put(s, SPLIT_AT, "w1e", _stack(i["L1_ffn_w1"][x]), x * 128)
        put(p, PLAIN_AT, "w2e", i["L1_ffn_w2"][x], x * F)
        put(p, PLAIN_AT, "b1e", i["L1_ffn_b1"][x][:, None], x)
        for part in range(2):
            e[part * E1 + x, EXACT_AT["sel_e"][0] + x] = 1
    put(p, PLAIN_AT, "b2e", _stack(i["L1_ffn_b2"]))
    put(p, PLAIN_AT, "gwe", _stack(i["L1_ffn_gate_w"]))
    row = {"bias_conv": i["L0_tok_bias"], "gbc": i["L0_ffn_gb"], "gbe": i["L1_ffn_gate_b"], "gamma": i["L1_ffn_gamma"],
           "beta": i["L1_ffn_beta"], "alpha": i["L0_tok_alpha"].reshape(1), "tau": i["L0_tok_tau"].reshape(1),
           "scale": i["L0_tok_scale"].reshape(1), "rank_c": np.arange(E0, 0, -1), "rank_e": np.arange(E1, 0, -1)}
    for name, a in row.items():
        put(p, PLAIN_AT, name, np.tile(np.asarray(a)[None, :], (128, 1)))
    put(p, PLAIN_AT, "ident", np.eye(128))
    u, t = np.arange(128)[:, None], np.arange(L)[None, :]
    put(p, PLAIN_AT, "causal", u <= t)
    put(p, PLAIN_AT, "band", (u >= t) & (u < t + TAPS))
    r = np.arange(128)
    c = np.arange(32)
    put(p, PLAIN_AT, "ones_bd", (r[:, None] // 64) == (c[None, :] // 8) % 2)
    put(p, PLAIN_AT, "window", ((r[:, None] // 16) % 2) == np.arange(2)[None, :])
    put(p, PLAIN_AT, "head", ((r[:, None] % 64) // HD) == np.arange(NH1)[None, :])
    return s, p, e


def kernel(**inputs):
    import concourse.bacc as bacc
    from concourse.bass_utils import run_bass_kernel_spmd

    i = {k: np.asarray(a) for k, a in inputs.items()}
    s, p, e = _layout(i)
    nc = bacc.Bacc("TRN2", target_bir_lowering=False, num_devices=1)
    arrays = {"x_dram": np.ascontiguousarray(i["x"]), "split_dram": s, "plain_dram": p, "exact_dram": e}
    args = [nc.dram_tensor(name, a.shape, F32, kind="ExternalInput").ap() for name, a in arrays.items()]
    out = nc.dram_tensor("out_dram", (B, L, F), F32, kind="ExternalOutput").ap()
    tower(nc, *args, out)
    r = run_bass_kernel_spmd(nc, [arrays], core_ids=[0])
    return r.results[0]["out_dram"]
```

```python
from contextlib import ExitStack

import numpy as np
import concourse.bass as bass
from concourse import mybir

F32 = mybir.dt.float32
F32R = mybir.dt.float32r
ALU = mybir.AluOpType
ACT = mybir.ActivationFunctionType
AX = mybir.AxisListType.X

B, LX, CIN, TAPS, F = 128, 125, 128, 9, 64
L = LX - TAPS + 1
G = 4
NG = B // G
N = G * L
GF = G * F
NH0 = 8
NP0 = NH0 // 2
E0, E1 = 4, 16
WS, NH1, HD = 64, 8, 8
NW = 2
W1N = L - WS
EPS = 1e-5
BIG = 3.0e38
TP = (TAPS + 1) // 2
LC = L + 1
A_, B_, C_, D_, E_ = range(5)
STAGES = 5

SPLIT = {"conv": TP * 128, "q0": NH0 * F, "w1c": (E0 + 1) * 128, "wq": 128, "wk": 128, "w1e": E1 * 128}
PLAIN = {"ident": 128, "causal": L, "band": L, "e0": NP0 * F, "gwc": E0, "w2c": E0 * F, "w2s": 128,
         "w3c": 3 * F, "eb3": F, "wv": 2 * F, "fold": 128, "wp": F, "ones_bd": 32, "gwe": E1, "w2e": E1 * F, "b2e": E1 // 2,
         "bias_conv": F, "gbc": E0, "gbe": E1, "gamma": F, "beta": F, "rank_c": E0, "rank_e": E1,
         "b1c": E0 + 1, "b2c": 3, "b3c": 1, "bp": 1, "b1e": E1, "window": 2, "head": NH1,
         "alpha": 1, "tau": 1, "scale": 1}
EXACT = {"sel_c": E0 * F, "sel_e": E1 * F, "query": 128, "rel": NH1 * WS}


def offsets(widths):
    at, out = 0, {}
    for name, n in widths.items():
        out[name] = (at, n)
        at += n
    return out, at


SPLIT_AT, NSPLIT = offsets(SPLIT)
PLAIN_AT, NPLAIN = offsets(PLAIN)
EXACT_AT, NEXACT = offsets(EXACT)


ORDER = {
    "pe": (
        "B.to_features.0 B.keys.0 B.query.0 D.to_features.0 B.query.1 B.query.2 E.to_features.0 D.window_q.0 "
        "D.window_k.0 E.gate.0 B.query.3 E.expert_in.0 B.omega.0 D.window_v.0 E.expert_in.1 D.score.0 B.zed.0 "
        "B.omega.1 D.flip.0 D.score.1 D.mix.0 E.weights.0 B.zed.1 E.expert_out.0 E.expert_in.2 B.omega.2 "
        "E.expert_out.1 D.flip.1 B.zed.2 D.score.2 E.expert_in.3 B.omega.3 D.mix.1 E.expert_out.2 E.expert_in.4 "
        "B.zed.3 D.flip.2 E.expert_out.3 B.r.0 D.score.3 E.expert_in.5 B.r_out.0 E.expert_out.4 C.to_features.0 "
        "D.mix.2 E.expert_in.6 C.gate.0 C.h1_shared.0 E.expert_out.5 D.flip.3 C.h1.0 E.expert_in.7 E.expert_out.6 "
        "C.h1.1 D.mix.3 C.h1.2 C.h1.3 E.expert_out.7 D.project.0 D.r_out.0 C.weights.0 A.conv_load.0 C.h2.0 "
        "E.residual.0 A.conv.0 C.h2.1 A.conv_out.0 C.h2_shared.0 C.mlp_out.0 C.r_out.0 "
    ),
    "act": (
        "D.center.0 E.center.0 B.to_features.0 C.center.0 D.normalise.0 B.keys.0 E.normalise.0 B.query.0 "
        "D.to_features.0 B.query.1 E.to_features.0 D.window_q.0 D.window_k.0 B.query.2 B.query.3 E.expert_in.0 "
        "D.window_v.0 E.top.0 E.expert_in.1 B.zed.0 D.score.0 D.flip.0 E.weights.0 D.score.1 B.zed.1 "
        "E.expert_out.0 D.flip.1 E.expert_in.2 E.expert_out.1 B.zed.2 E.expert_in.3 D.score.2 E.expert_out.2 "
        "E.expert_in.4 B.zed.3 D.flip.2 B.r.0 E.expert_out.3 C.normalise.0 E.expert_in.5 E.expert_out.4 "
        "C.to_features.0 E.expert_in.6 D.score.3 C.h1_shared.0 C.soft.0 E.expert_out.5 C.h1.0 E.expert_in.7 "
        "E.expert_out.6 D.flip.3 C.top.0 C.h1.1 C.h1.2 C.h1.3 E.expert_out.7 D.project.0 C.weights.0 "
        "A.conv_load.0 C.h2.0 E.center2.0 A.conv_fold.0 C.h2.1 C.h2_shared.0 A.center.0 C.mlp_out.0 A.normalise.0 "
    ),
    "dve": (
        "D.center.0 E.center.0 D.variance.0 C.center.0 E.variance.0 D.normalise.0 E.normalise.0 C.variance.0 "
        "C.normalise.0 E.gate.0 E.top.0 B.omega.0 D.score.0 E.weights.0 B.omega.1 D.score.1 D.mix.0 "
        "E.expert_out.0 B.omega.2 D.score.2 E.expert_out.1 B.omega.3 D.mix.1 E.expert_out.2 E.expert_out.3 "
        "B.r_out.0 D.score.3 E.expert_out.4 D.mix.2 C.gate.0 C.soft.0 E.expert_out.5 C.top.0 E.expert_out.6 "
        "D.mix.3 C.weights.0 E.expert_out.7 D.r_out.0 A.conv_load.0 E.residual.0 A.conv.0 C.h2.0 E.center2.0 "
        "E.variance2.0 A.conv_fold.0 C.h2.1 A.conv_out.0 A.center.0 A.variance.0 E.normalise2.0 C.r_out.0 "
        "A.normalise.0 "
    ),
    "pool": (
        "D.variance.0 E.variance.0 D.normalise.0 E.normalise.0 C.variance.0 D.window_k.0 E.weights.0 "
        "C.normalise.0 E.expert_out.0 E.expert_out.1 E.expert_out.2 E.expert_out.3 E.expert_out.4 E.expert_out.5 "
        "E.expert_out.6 C.weights.0 E.expert_out.7 A.conv.0 E.variance2.0 A.variance.0 A.normalise.0 "
    ),
}


def schedule(name, active):
    for word in ORDER[name].split():
        s, step, k = word.split(".")
        if "ABCDE".index(s) in active:
            yield step, "ABCDE".index(s), int(k)


class Counts:

    def __init__(self, eng, it):
        self.eng, self.it, self.known = eng, it, {}

    def __call__(self, s, per=1, more=None):
        more = per if more is None else more
        if isinstance(self.it, int):
            return per * (self.it - s) + more
        key = (per, more - per * s)
        if key not in self.known:
            self.known[key] = self.eng.snap(self.it * per + (more - per * s))
        return self.known[key]

    def before(self, s, per=1):
        return self(s, per, 0)

    def started(self, s):
        return not isinstance(self.it, int) or self.it >= s

    def most(self, s, now):
        return min(self.it - s + now, NG) if isinstance(self.it, int) else self(s, 1, now)


def tower(nc, x, split_w, plain_w, exact_w, out):
    with ExitStack() as ctx:
        def sb(name, shape, dt=F32):
            return ctx.enter_context(nc.sbuf_tensor(name, shape, dt))

        def sem(name):
            return ctx.enter_context(nc.semaphore(name))

        h_all = sb("h_all", [128, B * F])
        split_in = h_all[:, 0:NSPLIT]
        exact_in = h_all[:, NSPLIT:NSPLIT + NEXACT]
        split_hi = sb("split_hi", [128, NSPLIT], F32R)
        split_lo = sb("split_lo", [128, NSPLIT], F32R)
        plain = sb("plain", [128, NPLAIN])
        exact = sb("exact", [128, NEXACT], F32R)
        neg_alpha = sb("neg_alpha", [128, 1])
        alpha_tau = sb("alpha_tau", [128, 1])
        minus_half = sb("minus_half", [128, G])
        half = sb("half", [128, G])
        eps_tile = sb("eps_tile", [128, G])

        def hi(name, a=0, n=None):
            at, w = SPLIT_AT[name]
            return split_hi[:, at + a:at + a + (n or w)]

        def lo(name, a=0, n=None):
            at, w = SPLIT_AT[name]
            return split_lo[:, at + a:at + a + (n or w)]

        def pl(name, a=0, n=None, rows=slice(0, 128)):
            at, w = PLAIN_AT[name]
            return plain[rows, at + a:at + a + (n or w)]

        def ex(name, a=0, n=None):
            at, w = EXACT_AT[name]
            return exact[:, at + a:at + a + (n or w)]

        tok = slice(0, L)
        x_in = sb("x_in", [128, G * CIN])
        x_sq = sb("x_sq", [128, G * CIN])
        x_hi = sb("x_hi", [128, G * LX], F32R)
        x_lo = sb("x_lo", [128, G * LX], F32R)
        sq_sum = sb("sq_sum", [128, G])
        energy = sb("energy", [128, G])
        norm = sb("norm", [128, G])
        gate_exp = sb("gate_exp", [128, G])
        gate_den = sb("gate_den", [128, G])
        gate_all = sb("gate_all", [128, G])
        gate_inv = sb("gate_inv", [128, G])
        gate_tok = sb("gate_tok", [128, G])
        conv_odd = x_sq[0:64, 0:N]
        conv_t = conv_odd
        LN = range(B_, E_ + 2)
        total = {s: sb(f"total{s}", [128, G]) for s in LN}
        centered = {s: sb(f"centered{s}", [128, GF]) for s in LN}
        var = {s: sb(f"var{s}", [128, G]) for s in LN}
        var_eps = {s: sb(f"var_eps{s}", [128, G]) for s in LN}
        rstd = {s: sb(f"rstd{s}", [128, G]) for s in LN}
        normed = {s: sb(f"normed{s}", [128, GF]) for s in LN}
        squares = normed
        parts = {s: sb(f"parts{s}", [128, G * 128], F32R) for s in range(B_, E_ + 1)}
        feats = {s: sb(f"feats{s}", [128, N], F32R) for s in range(B_, E_ + 1)}
        keys = [sb(f"keys{i}", [128, N]) for i in range(2)]
        queries = sb("queries", [128, G * NP0 * L])
        omega = sb("omega", [128, 2 * NP0 * L])
        zed = sb("zed", [128, NP0 * N])
        result = {B_: omega[:, 0:2 * L]}
        NE = {C_: E0, E_: E1}
        logit = {s: sb(f"logit{s}", [128, G * NE[s]]) for s in NE}
        logit2 = {s: sb(f"logit2{s}", [128, G * NE[s]]) for s in NE}
        equal = {s: sb(f"equal{s}", [128, G * NE[s]]) for s in NE}
        first = {s: sb(f"first{s}", [128, G * NE[s]]) for s in NE}
        second = {s: sb(f"second{s}", [128, G * NE[s]]) for s in NE}
        best = {s: sb(f"best{s}", [128, G]) for s in NE}
        next_best = {s: sb(f"next_best{s}", [128, G]) for s in NE}
        rank = {s: sb(f"rank{s}", [128, G]) for s in NE}
        gap = {s: sb(f"gap{s}", [128, G]) for s in NE}
        gap_exp = {s: sb(f"gap_exp{s}", [128, G]) for s in NE}
        w_first = {s: sb(f"w_first{s}", [128, G]) for s in NE}
        w_second = {s: sb(f"w_second{s}", [128, G]) for s in NE}
        weight = {s: sb(f"weight{s}", [128, G * NE[s]]) for s in NE}
        w_parts = {s: sb(f"w_parts{s}", [128, G * 2 * NE[s]], F32R) for s in NE}
        w_feats = {s: sb(f"w_feats{s}", [128, N], F32R) for s in NE}
        prob_in = sb("prob_in", [128, G * E0])
        prob_exp = sb("prob_exp", [128, G * E0])
        prob_sum = sb("prob_sum", [128, G])
        prob = sb("prob", [128, G * E0])
        hid1 = sb("hid1", [128, (E0 + 1) * N])
        hid2 = sb("hid2", [128, 3 * N])
        result[C_] = hid1[:, 0:2 * L]
        q_bd = sb("q_bd", [128, G * NW * WS])
        k_win = sb("k_win", [128, G * WS])
        k_head = sb("k_head", [128, G * NH1 * WS])
        v_bd = sb("v_bd", [128, G * 4 * 32])
        neg_max = sb("neg_max", [128, NH1])
        probs = sb("probs", [128, NH1 * WS])
        shifted = probs
        probs_t = sb("probs_t", [128, NH1 * WS])
        result[D_] = probs_t[:, 0:2 * L]
        inv_sum = sb("inv_sum", [128, 128])
        mixed = sb("mixed", [128, G * 128])
        hid_e = [sb(f"hid_e{i}", [128, N]) for i in range(4)]
        pair_out = [sb(f"pair_out{i}", [128, N]) for i in range(4)]
        moe = sb("moe", [128, N])
        y_res = normed[E_ + 1]
        y_out = sb("y_out", [128, GF])

        bank = [ctx.enter_context(nc.psum_tensor(f"bank{i}", [128, 512], F32)) for i in range(8)]

        weights_in = sem("weights_in")
        exact_loaded = sem("exact_loaded")
        hi_made = sem("hi_made")
        weights_split = sem("weights_split")
        exact_made = sem("exact_made")
        setup_done = sem("setup_done")
        x_loaded = sem("x_loaded")
        x_turned = sem("x_turned")
        x_hi_made = sem("x_hi_made")
        x_lo_made = sem("x_lo_made")
        x_squared = sem("x_squared")
        sq_summed = sem("sq_summed")
        energy_sum = sem("energy_sum")
        energy_read = sem("energy_read")
        norm_made = sem("norm_made")
        gate_exp_made = sem("gate_exp_made")
        conv_done = sem("conv_done")
        conv_odd_made = sem("conv_odd_made")
        conv_folded = sem("conv_folded")
        conv_turned = sem("conv_turned")
        h_ready = {A_: sem("h_conv"), B_: sem("h_causal"), C_: sem("h_mlp"), D_: sem("h_window")}
        ln_centered = {s: sem(f"ln_centered{s}") for s in LN}
        ln_squared = {s: sem(f"ln_squared{s}") for s in LN}
        ln_var = {s: sem(f"ln_var{s}") for s in LN}
        ln_rstd = {s: sem(f"ln_rstd{s}") for s in LN}
        st = range(B_, E_ + 1)
        ln_normed = {s: sem(f"ln_normed{s}") for s in st}
        parts_hi = {s: sem(f"parts_hi{s}") for s in st}
        parts_lo = {s: sem(f"parts_lo{s}") for s in st}
        feats_psum = {s: sem(f"feats_psum{s}") for s in st}
        feats_made = {s: sem(f"feats_made{s}") for s in st}
        keys_psum = sem("keys_psum")
        keys_made = sem("keys_made")
        q_psum = sem("q_psum")
        q_made = sem("q_made")
        om_psum = [sem(f"om_psum{i}") for i in range(2)]
        om_masked = [sem(f"om_masked{i}") for i in range(2)]
        z_psum = sem("z_psum")
        z_made = sem("z_made")
        res_psum = {s: sem(f"res_psum{s}") for s in (B_, C_, D_)}
        res_made = {s: sem(f"res_made{s}") for s in (B_, C_, D_)}
        res_turned = {s: sem(f"res_turned{s}") for s in (B_, C_, D_)}
        lg_psum = {s: sem(f"lg_psum{s}") for s in NE}
        lg_read = {s: sem(f"lg_read{s}") for s in NE}
        gap_made = {s: sem(f"gap_made{s}") for s in NE}
        gap_exp_made = {s: sem(f"gap_exp_made{s}") for s in NE}
        weight_made = {s: sem(f"weight_made{s}") for s in NE}
        w_hi_made = {s: sem(f"w_hi_made{s}") for s in NE}
        w_lo_made = {s: sem(f"w_lo_made{s}") for s in NE}
        w_psum = {s: sem(f"w_psum{s}") for s in NE}
        w_feats_made = {s: sem(f"w_feats_made{s}") for s in NE}
        prob_shifted = sem("prob_shifted")
        prob_exp_made = sem("prob_exp_made")
        h1s_psum = sem("h1s_psum")
        h1s_made = sem("h1s_made")
        h1_psum = sem("h1_psum")
        h1_made = sem("h1_made")
        h2_psum = [sem("h2_psum0"), sem("h2_psum1"), sem("h2_psum_shared")]
        relu2_made = [sem("relu2_made0"), sem("relu2_made1")]
        h2_made = [sem("h2_made0"), sem("h2_made1"), sem("h2_made_shared")]
        wq_psum, wk_psum, wv_psum = sem("wq_psum"), sem("wk_psum"), sem("wv_psum")
        wq_made, wk_made, wv_made = sem("wq_made"), sem("wk_made"), sem("wv_made")
        k_masked = sem("k_masked")
        s_psum = sem("s_psum")
        s_shifted = sem("s_shifted")
        p_made = sem("p_made")
        pt_psum = sem("pt_psum")
        pt_made = sem("pt_made")
        u_psum = sem("u_psum")
        u_made = sem("u_made")
        e_psum = [sem(f"e_psum{i}") for i in range(4)]
        e_relu = [sem(f"e_relu{i}") for i in range(4)]
        e_out = [sem(f"e_out{i}") for i in range(2)]
        e_taken = [sem(f"e_taken{i}") for i in range(2)]
        e_weighted = [sem(f"e_weighted{i}") for i in range(2)]
        e_added = [sem(f"e_added{i}") for i in range(2)]
        moe_turned = sem("moe_turned")
        out_made = sem("out_made")
        out_stored = sem("out_stored")

        def hg(it, s):
            return h_all[tok, bass.ds((it - s) * GF, GF)]

        def norm_of(s):
            return max(s, B_)

        def per_seq(ap):
            return ap.rearrange("p (b f) -> p b f", b=G)

        def over_f(ap, n=F):
            return ap.unsqueeze(2).to_broadcast([L, G, n])

        def over_b(ap, n):
            return ap.unsqueeze(1).to_broadcast([L, G, n])

        def run(eng, name, steps):
            def iteration(it, active):
                n = Counts(eng, it)
                for step, s, k in schedule(name, active):
                    if step in steps:
                        steps[step](n, it, s, k)

            for t in range(STAGES):
                iteration(t, range(0, t + 1))
            with eng.Fori(STAGES, NG) as it:
                iteration(it, range(STAGES))
            for t in range(NG, NG + STAGES - 1):
                iteration(t, range(t - NG + 1, STAGES))

        block = ctx.enter_context(nc.Block())

        @block.sync
        def _(sp):
            sp.dma_start(split_in[:], split_w).then_inc(weights_in, 16)
            sp.dma_start(plain[:], plain_w).then_inc(weights_in, 16)
            sp.dma_start(exact_in[:, 0:NEXACT], exact_w).then_inc(exact_loaded, 16)

            def load(n, it, s, k):
                sp.wait_ge(x_turned, n.before(A_))
                sp.wait_ge(x_squared, n.before(A_))
                sp.dma_start(x_in[0:LX, :].rearrange("t (b c) -> t b c", b=G),
                             x[bass.ds((it - A_) * G, G), :, :].rearrange("b t c -> t b c")).then_inc(x_loaded, 16)

            def store(n, it, s, k):
                sp.wait_ge(out_made, n(E_))
                sp.dma_start(out[bass.ds((it - E_) * G, G), :, :].rearrange("b t f -> t b f"),
                             per_seq(y_out[tok, :])).then_inc(out_stored, 16)

            for t in range(STAGES):
                load(Counts(sp, t), t, A_, 0)
            store(Counts(sp, STAGES - 1), STAGES - 1, E_, 0)
            with sp.Fori(STAGES, NG) as it:
                n = Counts(sp, it)
                load(n, it, A_, 0)
                store(n, it, E_, 0)
            for t in range(NG, NG + STAGES - 1):
                store(Counts(sp, t), t, E_, 0)
            sp.wait_ge(out_stored, 16 * NG)

        @block.tensor
        def _(pe):
            mm = nc.tensor.matmul
            pe.wait_ge(setup_done, 2)
            ident = pl("ident")

            def to_features(n, it, s, k):
                to = {B_: bank[0], C_: bank[0], D_: bank[2], E_: bank[4]}[s]
                if s == B_ and n.started(C_):
                    pe.wait_ge(h_ready[C_], n.before(C_))
                elif s == C_:
                    pe.wait_ge(h_ready[B_], n.most(B_, 1))
                elif s == D_:
                    pe.wait_ge(h_ready[A_], n.most(A_, 0))
                pe.wait_ge(parts_lo[s], n(s))
                for b in range(G):
                    last = nc.tensor.transpose(to[:, b * L:(b + 1) * L], parts[s][tok, b * 128:(b + 1) * 128].bitcast(F32),
                                               ident[tok, 0:L])
                last.then_inc(feats_psum[s], 1)

            def conv_load(n, it, s, k):
                pe.wait_ge(x_loaded, n(A_, 16))
                if n.started(D_):
                    pe.wait_ge(h_ready[D_], n(D_))
                else:
                    pe.wait_ge(h_ready[A_], n.before(A_))
                for b in range(G):
                    last = nc.tensor.transpose(bank[2][:, b * LX:(b + 1) * LX], x_in[0:LX, b * CIN:(b + 1) * CIN],
                                               ident[0:LX, 0:LX])
                last.then_inc(x_turned, 1)

            def conv(n, it, s, k):
                pe.wait_ge(x_lo_made, n(A_))
                pe.wait_ge(sq_summed, n(A_))
                mm(bank[2][tok, 0:G], pl("band", rows=slice(0, LX)), sq_sum[0:LX, :], start=True,
                   stop=True).then_inc(energy_sum, 1)
                xh = x_hi[:, :].rearrange("c (b t) -> c b t", b=G)
                xl = x_lo[:, :].rearrange("c (b t) -> c b t", b=G)
                for j in range(TP):
                    for i, (w, v) in enumerate(((hi, xh), (hi, xl), (lo, xh))):
                        last = mm(bank[3][:, 0:G * LC], w("conv", j * 128, 128), v[:, :, 2 * j:2 * j + LC] if 2 * j + LC <= LX
                                  else v[:, :, LX - LC:LX], start=(j == 0 and i == 0), stop=(j == TP - 1 and i == 2))
                last.then_inc(conv_done, 1)

            def conv_out(n, it, s, k):
                pe.wait_ge(conv_folded, n(A_))
                for b in range(G):
                    last = nc.tensor.transpose(bank[2][tok, b * 128:(b + 1) * 128], x_sq[:, b * L:(b + 1) * L], ident)
                last.then_inc(conv_turned, 1)

            def keys_step(n, it, s, k):
                pe.wait_ge(feats_made[B_], n(B_))
                mm(bank[1][:, 0:N], pl("fold"), feats[B_][:, :].bitcast(F32), start=True, stop=True).then_inc(keys_psum, 1)

            def query(n, it, s, p):
                if p == 1:
                    pe.wait_ge(keys_made, n(B_))
                elif p >= 2:
                    pe.wait_ge(q_made, n(B_, 4, p - 1))
                to = bank[p % 2][:, 0:N]
                mm(to, hi("q0", p * 128, 128), feats[B_][:, :], start=True, stop=False)
                mm(to, lo("q0", p * 128, 128), feats[B_][:, :], start=False, stop=True).then_inc(q_psum, 1)

            def omega_bank(b, par):
                return bank[(b + par) % 2]

            def omega_step(n, it, s, b):
                for par in range(2):
                    if b == 0 and par == 0:
                        pe.wait_ge(q_made, n(B_, 4))
                    if b > 0 and par == 0:
                        pe.wait_ge(om_masked[1], n(B_, 4, b))
                    if b > 0 and par == 1:
                        pe.wait_ge(z_made, n(B_, 4, b))
                    to = omega_bank(b, par)[tok, 0:NP0 * L]
                    mm(to, keys[par][:, b * L:(b + 1) * L], queries[:, b * NP0 * L:(b + 1) * NP0 * L], start=True,
                       stop=True).then_inc(om_psum[par], 1)

            def zed_step(n, it, s, b):
                pe.wait_ge(om_masked[0], n(B_, 4, b + 1))
                pe.wait_ge(om_masked[1], n(B_, 4, b + 1))
                for par in range(2):
                    last = mm(omega_bank(b, 0)[64 * par:64 * par + 64, 0:NP0 * L], normed[B_][tok, b * F:(b + 1) * F],
                              omega[tok, par * NP0 * L:(par + 1) * NP0 * L], start=True, stop=True)
                last.then_inc(z_psum, 1)

            def r_step(n, it, s, k):
                pe.wait_ge(z_made, n(B_, 4))
                for p in range(NP0):
                    for half_ in range(2):
                        last = mm(bank[0][64 * half_:64 * half_ + 64, 0:2 * L], pl("e0", p * F, F),
                                  zed[:, p * N + half_ * 2 * L:p * N + (half_ + 1) * 2 * L],
                                  start=(p == 0), stop=(p == NP0 - 1))
                last.then_inc(res_psum[B_], 1)

            def r_out(n, it, s, k):
                to = {B_: bank[1], C_: bank[0], D_: bank[3]}[s]
                pe.wait_ge(res_made[s], n(s))
                for j in range(2):
                    last = nc.tensor.transpose(to[tok, j * 128:(j + 1) * 128], result[s][:, j * L:(j + 1) * L], ident)
                last.then_inc(res_turned[s], 1)

            def gate(n, it, s, k):
                to = bank[1] if s == C_ else bank[5]
                pe.wait_ge(feats_made[s], n(s))
                for b in range(G):
                    last = mm(to[tok, b * NE[s]:(b + 1) * NE[s]], feats[s][:, b * L:(b + 1) * L].bitcast(F32),
                              pl("gwc" if s == C_ else "gwe"), start=True, stop=True)
                last.then_inc(lg_psum[s], 1)

            def weights(n, it, s, k):
                to = bank[1] if s == C_ else bank[6]
                m = 2 * NE[s]
                if s == C_:
                    pe.wait_ge(h1_made, n(C_, 4, 3))
                pe.wait_ge(w_lo_made[s], n(s))
                for b in range(G):
                    last = nc.tensor.transpose(to[0:m, b * L:(b + 1) * L], w_parts[s][tok, b * m:(b + 1) * m].bitcast(F32),
                                               ident[tok, 0:L])
                last.then_inc(w_psum[s], 1)

            def two_pass(to, name, at, v):
                mm(to, hi(name, at, 128), v, start=True, stop=False)
                return mm(to, lo(name, at, 128), v, start=False, stop=True)

            def h1_shared(n, it, s, k):
                two_pass(bank[0][:, 0:N], "w1c", E0 * 128, feats[C_][:, :]).then_inc(h1s_psum, 1)

            def h1(n, it, s, e):
                if e == 0:
                    pe.wait_ge(lg_read[C_], n(C_))
                elif e == 1:
                    pe.wait_ge(h1s_made, n(C_))
                else:
                    pe.wait_ge(h1_made, n(C_, 4, e - 1))
                two_pass(bank[1 - e % 2][:, 0:N], "w1c", e * 128, feats[C_][:, :]).then_inc(h1_psum, 1)

            def h2(n, it, s, p):
                if p == 0:
                    pe.wait_ge(h1_made, n(C_, 4))
                    pe.wait_ge(w_feats_made[C_], n(C_))
                else:
                    pe.wait_ge(relu2_made[0], n(C_))
                for i in range(2):
                    last = mm(bank[0][64 * i:64 * i + 64, 0:N], pl("w2c", (2 * p + i) * F, F),
                              hid1[:, (2 * p + i) * N:(2 * p + i + 1) * N], start=True, stop=True)
                if p == 1:
                    pe.wait_ge(h2_made[0], n(C_))
                mm(bank[1][:, 0:N], ex("sel_c", p * 128, 128), w_feats[C_][:, :], start=True,
                   stop=True).then_inc(h2_psum[p], 1)

            def h2_shared(n, it, s, k):
                pe.wait_ge(relu2_made[1], n(C_))
                mm(bank[0][:, 0:N], pl("w2s"), hid1[:, E0 * N:(E0 + 1) * N], start=True,
                   stop=True).then_inc(h2_psum[2], 1)

            def mlp_out(n, it, s, k):
                pe.wait_ge(h2_made[1], n(C_))
                pe.wait_ge(h2_made[2], n(C_))
                for i in range(4):
                    for half_ in range(2):
                        cols = slice(half_ * 2 * L, (half_ + 1) * 2 * L)
                        v = hid2[:, i * N:(i + 1) * N][:, cols] if i < 3 else w_feats[C_][:, cols].bitcast(F32)
                        w = pl("w3c", i * F, F) if i < 3 else pl("eb3")
                        last = mm(bank[1][64 * half_:64 * half_ + 64, 0:2 * L], w, v, start=(i == 0), stop=(i == 3))
                last.then_inc(res_psum[C_], 1)

            def window_q(n, it, s, k):
                pe.wait_ge(feats_made[D_], n(D_))
                two_pass(bank[3][:, 0:N], "wq", 0, feats[D_][:, :]).then_inc(wq_psum, 1)

            def window_k(n, it, s, k):
                two_pass(bank[2][:, 0:N], "wk", 0, feats[D_][:, :]).then_inc(wk_psum, 1)

            def window_v(n, it, s, k):
                pe.wait_ge(wq_made, n(D_))
                for b in range(G):
                    last = mm(bank[3][tok, b * 128:(b + 1) * 128], feats[D_][:, b * L:(b + 1) * L].bitcast(F32), pl("wv"),
                              start=True, stop=True)
                last.then_inc(wv_psum, 1)

            def score(n, it, s, b):
                if b == 0:
                    pe.wait_ge(k_masked, n(D_))
                else:
                    pe.wait_ge(s_shifted, n(D_, 4, b))
                mm(bank[2][:, :], q_bd[:, b * 128:(b + 1) * 128], k_head[:, b * 512:(b + 1) * 512], start=True, stop=False)
                mm(bank[2][:, :], ex("query"), ex("rel"), start=False, stop=True).then_inc(s_psum, 1)

            def flip(n, it, s, b):
                pe.wait_ge(p_made, n(D_, 4, b + 1))
                if b == 0:
                    pe.wait_ge(wv_made, n(D_))
                else:
                    pe.wait_ge(u_made, n(D_, 4, b))
                for p in range(4):
                    last = nc.tensor.transpose(bank[3][:, p * 128:(p + 1) * 128], probs[:, p * 128:(p + 1) * 128], ident)
                last.then_inc(pt_psum, 1)

            def mix(n, it, s, b):
                pe.wait_ge(pt_made, n(D_, 4, b + 1))
                for at, w in ((0, None), (128, pl("ones_bd"))):
                    for p in range(4):
                        v = v_bd[:, (b * 4 + p) * 32:(b * 4 + p + 1) * 32] if w is None else w
                        last = mm(bank[3][32 * p:32 * p + 32, at:at + 128], v, probs_t[:, p * 128:(p + 1) * 128],
                                  start=True, stop=True)
                last.then_inc(u_psum, 1)

            def project(n, it, s, k):
                pe.wait_ge(u_made, n(D_, 4))
                for half_ in range(2):
                    last = mm(bank[2][64 * half_:64 * half_ + 64, 0:2 * L], pl("wp"),
                              mixed[:, :].rearrange("p (b q) -> p b q", b=G)[:, 2 * half_:2 * half_ + 2, tok],
                              start=True, stop=True)
                last.then_inc(res_psum[D_], 1)

            def expert_in(n, it, s, j):
                if j == 0:
                    pe.wait_ge(lg_read[E_], n(E_))
                for e in (2 * j, 2 * j + 1):
                    if j:
                        pe.wait_ge(e_relu[(e - 2) % 4], n(E_, 4, (e - 2) // 4 + 1))
                    two_pass(bank[4 + e % 2][:, 0:N], "w1e", e * 128, feats[E_][:, :]).then_inc(e_psum[e % 4], 1)

            def expert_out(n, it, s, j):
                if j == 0:
                    pe.wait_ge(w_feats_made[E_], n(E_))
                else:
                    pe.wait_ge(e_weighted[(j - 1) % 2], n(E_, 4, (j - 1) // 2 + 1))
                mm(bank[6][:, 0:N], ex("sel_e", j * 128, 128), w_feats[E_][:, :], start=True, stop=True)
                for i in range(2):
                    e = 2 * j + i
                    pe.wait_ge(e_relu[e % 4], n(E_, 4, e // 4 + 1))
                    last = mm(bank[7][64 * i:64 * i + 64, 0:N], pl("w2e", e * F, F), hid_e[e % 4][:, :],
                              start=True, stop=True)
                last.then_inc(e_out[j % 2], 1)

            def residual(n, it, s, k):
                pe.wait_ge(e_added[1], n(E_, 4))
                for b in range(G):
                    last = nc.tensor.transpose(bank[4][tok, b * 128:(b + 1) * 128], moe[:, b * L:(b + 1) * L], ident)
                last.then_inc(moe_turned, 1)

            run(pe, "pe", {"to_features": to_features, "conv_load": conv_load, "conv": conv, "conv_out": conv_out,
                           "keys": keys_step, "query": query, "omega": omega_step, "zed": zed_step, "r": r_step, "r_out": r_out,
                           "gate": gate, "weights": weights, "h1_shared": h1_shared, "h1": h1, "h2": h2,
                           "h2_shared": h2_shared, "mlp_out": mlp_out, "window_q": window_q, "window_k": window_k,
                           "window_v": window_v, "score": score, "flip": flip, "mix": mix, "project": project,
                           "expert_in": expert_in, "expert_out": expert_out,
                           "residual": residual})

        @block.scalar
        def _(act):
            fn = nc.scalar.activation
            act.wait_ge(weights_in, 32)
            at = SPLIT_AT["wq"][0]
            fn(split_in[:, at:at + 128], split_in[:, at:at + 128], ACT.Copy, scale=float(HD) ** -0.5)
            nc.scalar.drain()
            fn(split_hi[:, :], split_in[:, :], ACT.Copy).then_inc(hi_made, 1)
            act.wait_ge(exact_loaded, 16)
            fn(exact[:, :], exact_in[:, 0:NEXACT], ACT.Copy).then_inc(exact_made, 1)
            act.wait_ge(exact_made, 1)
            act.wait_ge(setup_done, 2)

            def center(n, it, s, k):
                y = norm_of(s)
                act.wait_ge(ln_centered[y], n(min(s, E_)))
                if s <= E_:
                    act.wait_ge(parts_lo[y], n.before(s))
                if s == A_:
                    act.wait_ge(z_psum, n(A_, 4, 0))
                if s == E_:
                    act.wait_ge(ln_centered[s + 1], n.before(E_))
                fn(squares[y][tok, :], centered[y][tok, :], ACT.Square,
                   scale=float(F) ** -0.5).then_inc(ln_squared[y], 1)

            def normalise(n, it, s, k):
                y = norm_of(s)
                act.wait_ge(ln_normed[y], n(s))
                act.wait_ge(feats_psum[y], n.before(s))
                fn(parts[y][tok, :].rearrange("p (b c f) -> p b c f", b=G, c=2)[:, :, 0, :], per_seq(normed[y][tok, :]),
                   ACT.Copy).then_inc(parts_hi[y], 1)

            def to_features(n, it, s, k):
                frm = {B_: bank[0], C_: bank[0], D_: bank[2], E_: bank[4]}[s]
                act.wait_ge(feats_psum[s], n(s))
                fn(feats[s][:, :], frm[:, 0:N], ACT.Copy).then_inc(feats_made[s], 1)

            def conv_load(n, it, s, k):
                act.wait_ge(x_loaded, n(A_, 16))
                act.wait_ge(conv_turned, n.before(A_))
                fn(x_sq[0:LX, :], x_in[0:LX, :], ACT.Square).then_inc(x_squared, 1)
                act.wait_ge(x_turned, n(A_))
                act.wait_ge(conv_done, n.before(A_))
                fn(x_hi[:, :], bank[2][:, 0:G * LX], ACT.Copy).then_inc(x_hi_made, 1)

            def conv_fold(n, it, s, k):
                act.wait_ge(norm_made, n(A_))
                fn(gate_exp[tok, :], norm[tok, :], ACT.Exp, scale=neg_alpha[tok, :], bias=alpha_tau[tok, :])\
                    .then_inc(gate_exp_made, 1)
                act.wait_ge(sq_summed, n(A_))
                act.wait_ge(conv_done, n(A_))
                fn(conv_odd[:, :].rearrange("f (b t) -> f b t", b=G),
                   bank[3][64:128, 0:G * LC].rearrange("f (b t) -> f b t", b=G)[:, :, 1:LC], ACT.Copy)\
                    .then_inc(conv_odd_made, 1)

            def keys_step(n, it, s, k):
                act.wait_ge(keys_psum, n(B_))
                act.wait_ge(om_psum[1], n(B_, 4, 0))
                fn(keys[0][0:64, :], bank[1][0:64, 0:N], ACT.Copy)
                fn(keys[1][64:128, :], bank[1][64:128, 0:N], ACT.Copy).then_inc(keys_made, 1)

            def query(n, it, s, p):
                act.wait_ge(q_psum, n(B_, 4, p + 1))
                fn(queries[:, :].rearrange("j (b p t) -> j b p t", b=G, p=NP0)[:, :, p, :],
                   bank[p % 2][:, 0:N].rearrange("j (b t) -> j b t", b=G), ACT.Copy).then_inc(q_made, 1)

            def zed_step(n, it, s, b):
                act.wait_ge(z_psum, n(B_, 4, b + 1))
                if b == 0:
                    act.wait_ge(res_psum[B_], n.before(B_))
                fn(zed[:, :].rearrange("j (p b t) -> j p b t", p=NP0, b=G)[:, :, b, :],
                   bank[b % 2][:, 0:NP0 * L].rearrange("j (p t) -> j p t", p=NP0), ACT.Copy).then_inc(z_made, 1)

            def take_result(n, s, frm, bias):
                act.wait_ge(res_psum[s], n(s))
                act.wait_ge(res_turned[s], n.before(s))
                if bias is None:
                    fn(result[s][:, :], frm[:, 0:2 * L], ACT.Copy).then_inc(res_made[s], 1)
                else:
                    fn(result[s][:, :], frm[:, 0:2 * L], ACT.Identity, bias=bias).then_inc(res_made[s], 1)

            def r_step(n, it, s, k):
                take_result(n, B_, bank[0], None)

            def mlp_out(n, it, s, k):
                take_result(n, C_, bank[1], pl("b3c"))

            def project(n, it, s, k):
                take_result(n, D_, bank[2], pl("bp"))

            def soft(n, it, s, k):
                act.wait_ge(prob_shifted, n(C_))
                fn(prob_exp[tok, :], prob_in[tok, :], ACT.Exp).then_inc(prob_exp_made, 1)

            def top(n, it, s, k):
                act.wait_ge(gap_made[s], n(s))
                fn(gap_exp[s][tok, :], gap[s][tok, :], ACT.Exp).then_inc(gap_exp_made[s], 1)

            def weights(n, it, s, k):
                act.wait_ge(weight_made[s], n(s))
                act.wait_ge(w_psum[s], n.before(s))
                fn(w_parts[s][tok, :].rearrange("p (b c e) -> p b c e", b=G, c=2)[:, :, 0, :],
                   weight[s][tok, :].rearrange("p (b e) -> p b e", b=G), ACT.Copy).then_inc(w_hi_made[s], 1)
                act.wait_ge(w_psum[s], n(s))
                frm = bank[1] if s == C_ else bank[6]
                fn(w_feats[s][0:2 * NE[s], :], frm[0:2 * NE[s], 0:N], ACT.Copy).then_inc(w_feats_made[s], 1)

            def h1_shared(n, it, s, k):
                act.wait_ge(h1s_psum, n(C_))
                fn(hid1[:, E0 * N:(E0 + 1) * N], bank[0][:, 0:N], ACT.Relu, bias=pl("b1c", E0, 1)).then_inc(h1s_made, 1)

            def h1(n, it, s, e):
                act.wait_ge(h1_psum, n(C_, 4, e + 1))
                if e == 0:
                    act.wait_ge(res_turned[C_], n.before(C_))
                fn(hid1[:, e * N:(e + 1) * N], bank[1 - e % 2][:, 0:N], ACT.Relu, bias=pl("b1c", e, 1)).then_inc(h1_made, 1)

            def h2(n, it, s, p):
                act.wait_ge(h2_psum[p], n(C_))
                if p == 0:
                    act.wait_ge(res_psum[C_], n.before(C_))
                fn(hid2[:, p * N:(p + 1) * N], bank[0][:, 0:N], ACT.Relu, bias=pl("b2c", p, 1)).then_inc(relu2_made[p], 1)

            def h2_shared(n, it, s, k):
                act.wait_ge(h2_psum[2], n(C_))
                fn(hid2[:, 2 * N:3 * N], bank[0][:, 0:N], ACT.Relu, bias=pl("b2c", 2, 1)).then_inc(h2_made[2], 1)

            def to_windows(dst, frm):
                v = frm[:, 0:N].rearrange("f (b t) -> f b t", b=G)
                fn(dst[0], v[0:64, :, 0:WS], ACT.Copy)
                return fn(dst[1], v[64:128, :, WS:L], ACT.Copy)

            def window_q(n, it, s, k):
                act.wait_ge(wq_psum, n(D_))
                v = q_bd[:, :].rearrange("f (b q) -> f b q", b=G)
                act.wait_ge(s_psum, n(D_, 4, 0))
                to_windows((v[0:64, :, 0:WS], v[64:128, :, WS:L]), bank[3]).then_inc(wq_made, 1)

            def window_k(n, it, s, k):
                act.wait_ge(wk_psum, n(D_))
                act.wait_ge(k_masked, n.before(D_))
                v = k_win[:, :].rearrange("f (b k) -> f b k", b=G)
                to_windows((v[0:64, :, 0:WS], v[64:128, :, 0:W1N]), bank[2]).then_inc(wk_made, 1)

            def window_v(n, it, s, k):
                act.wait_ge(wv_psum, n(D_))
                act.wait_ge(u_psum, n(D_, 4, 0))
                for w, rows in ((0, WS), (1, W1N)):
                    for h in range(2):
                        last = fn(v_bd[64 * h:64 * h + rows, :].rearrange("k (b x c) -> k b x c", b=G, c=32)
                                  [:, :, :, 16 * w + 8 * h:16 * w + 8 * h + 8],
                                  bank[3][64 * w:64 * w + rows, :].rearrange("k (b x c) -> k b x c", b=G, c=16)
                                  [:, :, 0:4, 8 * h:8 * h + 8], ACT.Copy)
                last.then_inc(wv_made, 1)

            def score(n, it, s, b):
                act.wait_ge(s_shifted, n(D_, 4, b + 1))
                fn(probs[:, :], shifted[:, :], ACT.Exp).then_inc(p_made, 1)

            def flip(n, it, s, b):
                act.wait_ge(pt_psum, n(D_, 4, b + 1))
                act.wait_ge(u_psum, n(D_, 4, b))
                if b == 0:
                    act.wait_ge(res_turned[D_], n.before(D_))
                fn(probs_t[:, :], bank[3][:, :], ACT.Copy).then_inc(pt_made, 1)

            def relu(n, e):
                act.wait_ge(e_psum[e % 4], n(E_, 4, e // 4 + 1))
                act.wait_ge(e_out[(e // 2) % 2], n(E_, 4, e // 4))
                fn(hid_e[e % 4][:, :], bank[4 + e % 2][:, 0:N], ACT.Relu, bias=pl("b1e", e, 1)).then_inc(e_relu[e % 4], 1)

            def expert_in(n, it, s, j):
                relu(n, 2 * j)
                relu(n, 2 * j + 1)

            def expert_out(n, it, s, j):
                act.wait_ge(e_out[j % 2], n(E_, 4, j // 2 + 1))
                act.wait_ge(e_added[j % 2], n(E_, 4, max(j // 2 - 1, 0)))
                fn(pair_out[j % 4][:, :], bank[7][:, 0:N], ACT.Identity, bias=pl("b2e", j, 1)).then_inc(e_taken[j % 2], 1)

            def center2(n, it, s, k):
                center(n, it, E_ + 1, k)

            run(act, "act", {"center": center, "normalise": normalise, "to_features": to_features,
                             "conv_load": conv_load, "conv_fold": conv_fold, "keys": keys_step, "query": query, "zed": zed_step,
                             "r": r_step, "mlp_out": mlp_out, "project": project, "soft": soft, "top": top,
                             "weights": weights, "h1_shared": h1_shared, "h1": h1, "h2": h2, "h2_shared": h2_shared,
                             "window_q": window_q, "window_k": window_k, "window_v": window_v, "score": score,
                             "flip": flip, "expert_in": expert_in, "expert_out": expert_out, "center2": center2})

        @block.vector
        def _(dve):
            v = nc.vector
            settle = nc.vector.drain

            dve.wait_ge(weights_in, 32)
            v.tensor_scalar(neg_alpha[:, :], pl("alpha"), -1.0, None, ALU.mult)
            v.tensor_tensor(alpha_tau[:, :], pl("alpha"), pl("tau"), ALU.mult)
            dve.wait_ge(hi_made, 1)
            v.tensor_tensor(split_lo[:, :], split_in[:, :], split_hi[:, :].bitcast(F32), ALU.subtract)\
                .then_inc(weights_split, 1)
            at, w = EXACT_AT["rel"]
            dve.wait_ge(exact_made, 1)
            v.tensor_tensor(exact[64:128, at:at + w], exact_in[64:128, at:at + w],
                            exact[64:128, at:at + w].bitcast(F32), ALU.subtract).then_inc(setup_done, 1)

            def center_of(n, s, src):
                v.tensor_reduce(total[s][tok, :], src, axis=AX, op=ALU.add)
                settle()
                v.scalar_tensor_tensor(out=per_seq(centered[s][tok, :]), in0=over_f(total[s][tok, :]), scalar=-1.0 / F,
                                       in1=src, op0=ALU.mult, op1=ALU.add).then_inc(ln_centered[s], 1)

            def center(n, it, s, k):
                y = norm_of(s)
                if s == A_:
                    settle()
                else:
                    dve.wait_ge(h_ready[y - 1], n(s))
                    v.nop()
                center_of(n, y, per_seq(hg(it, s)))

            def variance(n, it, s, k):
                y = norm_of(s)
                dve.wait_ge(ln_squared[y], n(min(s, E_)))
                v.tensor_reduce(var[y][tok, :], per_seq(squares[y][tok, :]), axis=AX, op=ALU.add).then_inc(ln_var[y], 1)

            def normalise(n, it, s, k):
                y = norm_of(s)
                dve.wait_ge(ln_rstd[y], n(s))
                dve.wait_ge(parts_lo[y], n.before(s))
                v.tensor_tensor(per_seq(normed[y][tok, :]), per_seq(centered[y][tok, :]), over_f(rstd[y][tok, :]),
                                ALU.mult).then_inc(ln_normed[y], 1)

            def conv_load(n, it, s, k):
                dve.wait_ge(x_squared, n(A_))
                v.tensor_reduce(sq_sum[0:LX, :], x_sq[0:LX, :].rearrange("t (b c) -> t b c", b=G), axis=AX, op=ALU.add)\
                    .then_inc(sq_summed, 1)
                dve.wait_ge(x_hi_made, n(A_))
                v.tensor_tensor(x_lo[:, :], bank[2][:, 0:G * LX], x_hi[:, :].bitcast(F32), ALU.subtract)\
                    .then_inc(x_lo_made, 1)

            def conv(n, it, s, k):
                dve.wait_ge(energy_sum, n(A_))
                v.tensor_scalar(energy[tok, :], bank[2][tok, 0:G], EPS, None, ALU.add).then_inc(energy_read, 1)

            def conv_fold(n, it, s, k):
                dve.wait_ge(gate_exp_made, n(A_))
                v.tensor_scalar(gate_den[tok, :], norm[tok, :], EPS, None, ALU.add)
                settle()
                v.scalar_tensor_tensor(out=gate_all[tok, :], in0=gate_exp[tok, :], scalar=1.0, in1=gate_den[tok, :],
                                       op0=ALU.add, op1=ALU.mult)
                settle()
                v.reciprocal(gate_inv[tok, :], gate_all[tok, :])
                settle()
                v.tensor_scalar(gate_tok[tok, :], gate_inv[tok, :], pl("scale", rows=tok), None, ALU.mult)
                dve.wait_ge(conv_odd_made, n(A_))
                v.tensor_tensor(conv_t[:, :].rearrange("f (b t) -> f b t", b=G),
                                bank[3][0:64, 0:G * LC].rearrange("f (b t) -> f b t", b=G)[:, :, tok],
                                conv_odd[:, :].rearrange("f (b t) -> f b t", b=G), ALU.add).then_inc(conv_folded, 1)

            def conv_out(n, it, s, k):
                dve.wait_ge(conv_turned, n(A_))
                v.tensor_tensor(per_seq(hg(it, A_)), bank[2][tok, :].rearrange("p (b f) -> p b f", b=G)[:, :, 0:F], over_f(gate_tok[tok, :]), ALU.mult)
                settle()
                v.tensor_tensor(per_seq(hg(it, A_)), per_seq(hg(it, A_)), over_b(pl("bias_conv", rows=tok), F),
                                ALU.add).then_inc(h_ready[A_], 1)

            def omega_step(n, it, s, b):
                dve.wait_ge(z_psum, n(B_, 4, b))
                if b == 0:
                    dve.wait_ge(res_turned[B_], n.before(B_))
                for par in range(2):
                    dve.wait_ge(om_psum[par], n(B_, 4, b + 1))
                    by_pair = lambda ap: ap.rearrange("u (p t) -> u p t", p=NP0)
                    v.tensor_tensor(by_pair(omega[tok, par * NP0 * L:(par + 1) * NP0 * L]),
                                    by_pair(bank[(b + par) % 2][tok, 0:NP0 * L]),
                                    pl("causal", rows=tok).unsqueeze(1).to_broadcast([L, NP0, L]), ALU.mult)\
                        .then_inc(om_masked[par], 1)

            def r_out(n, it, s, k):
                frm = {B_: bank[1], C_: bank[0], D_: bank[3]}[s]
                dve.wait_ge(res_turned[s], n(s))
                cut = lambda ap: ap.rearrange("p (h j f) -> p j h f", h=2, j=2)
                v.tensor_tensor(cut(hg(it, s)), frm[tok, 0:GF].rearrange("p (j h f) -> p j h f", h=2, j=2), cut(hg(it, s)),
                                ALU.add).then_inc(h_ready[s], 1)

            def seqs(ap):
                return ap.rearrange("p (b e) -> p b e", b=G)

            def gate(n, it, s, k):
                e = NE[s]
                frm = bank[1] if s == C_ else bank[5]
                dve.wait_ge(lg_psum[s], n(s))
                v.tensor_tensor(seqs(logit[s][tok, :]), seqs(frm[tok, 0:G * e]),
                                over_b(pl("gbc" if s == C_ else "gbe", rows=tok), e), ALU.add).then_inc(lg_read[s], 1)
                settle()
                if s == C_:
                    v.tensor_reduce(best[s][tok, :], seqs(logit[s][tok, :]), axis=AX, op=ALU.max, negate=True)
                    settle()
                    v.tensor_tensor(seqs(prob_in[tok, :]), seqs(logit[s][tok, :]), over_f(best[s][tok, :], e), ALU.add)\
                        .then_inc(prob_shifted, 1)

            def soft(n, it, s, k):
                dve.wait_ge(prob_exp_made, n(C_))
                v.tensor_reduce(prob_sum[tok, :], seqs(prob_exp[tok, :]), axis=AX, op=ALU.add)
                settle()
                v.reciprocal(rank[C_][tok, :], prob_sum[tok, :])
                settle()
                v.tensor_tensor(seqs(prob[tok, :]), seqs(prob_exp[tok, :]), over_f(rank[C_][tok, :], E0), ALU.mult)
                settle()

            def pick(s, frm, value, chosen):
                e = NE[s]
                v.tensor_reduce(value[tok, :], frm, axis=AX, op=ALU.max)
                settle()
                v.tensor_tensor(seqs(equal[s][tok, :]), frm, over_f(value[tok, :], e), ALU.is_equal)
                settle()
                v.tensor_tensor(seqs(equal[s][tok, :]), seqs(equal[s][tok, :]),
                                over_b(pl("rank_c" if s == C_ else "rank_e", rows=tok), e), ALU.mult)
                settle()
                v.tensor_reduce(rank[s][tok, :], seqs(equal[s][tok, :]), axis=AX, op=ALU.max)
                settle()
                v.tensor_tensor(seqs(chosen[tok, :]), seqs(equal[s][tok, :]), over_f(rank[s][tok, :], e), ALU.is_equal)
                settle()

            def top(n, it, s, k):
                src = prob if s == C_ else logit[s]
                pick(s, seqs(src[tok, :]), best[s], first[s])
                v.scalar_tensor_tensor(out=logit2[s][tok, :], in0=first[s][tok, :], scalar=-BIG, in1=src[tok, :],
                                       op0=ALU.mult, op1=ALU.add)
                settle()
                pick(s, seqs(logit2[s][tok, :]), next_best[s], second[s])
                v.tensor_tensor(gap[s][tok, :], next_best[s][tok, :], best[s][tok, :], ALU.subtract).then_inc(gap_made[s], 1)

            def weights(n, it, s, k):
                e = NE[s]
                dve.wait_ge(gap_exp_made[s], n(s))
                v.tensor_scalar(rank[s][tok, :], gap_exp[s][tok, :], 1.0, None, ALU.add)
                settle()
                v.reciprocal(w_first[s][tok, :], rank[s][tok, :])
                settle()
                v.tensor_tensor(w_second[s][tok, :], gap_exp[s][tok, :], w_first[s][tok, :], ALU.mult)
                v.tensor_tensor(seqs(first[s][tok, :]), seqs(first[s][tok, :]), over_f(w_first[s][tok, :], e), ALU.mult)
                settle()
                v.tensor_tensor(seqs(second[s][tok, :]), seqs(second[s][tok, :]), over_f(w_second[s][tok, :], e), ALU.mult)
                settle()
                v.tensor_tensor(weight[s][tok, :], first[s][tok, :], second[s][tok, :], ALU.add).then_inc(weight_made[s], 1)

            def h2(n, it, s, p):
                dve.wait_ge(relu2_made[p], n(C_))
                v.tensor_tensor(hid2[:, p * N:(p + 1) * N], hid2[:, p * N:(p + 1) * N], bank[1][:, 0:N], ALU.mult).then_inc(h2_made[p], 1)

            def score(n, it, s, b):
                dve.wait_ge(s_psum, n(D_, 4, b + 1))
                by_head = bank[2][:, :].rearrange("q (h k) -> q h k", h=NH1)
                v.tensor_reduce(neg_max[:, :], by_head, axis=AX, op=ALU.max, negate=True)
                settle()
                dve.wait_ge(pt_psum, n(D_, 4, b))
                v.tensor_tensor(shifted[:, :].rearrange("q (h k) -> q h k", h=NH1), by_head,
                                neg_max[:, :].unsqueeze(2).to_broadcast([128, NH1, WS]), ALU.add).then_inc(s_shifted, 1)

            def mix(n, it, s, b):
                dve.wait_ge(u_psum, n(D_, 4, b + 1))
                v.reciprocal(inv_sum[:, :], bank[3][:, 128:256])
                settle()
                if b == 0:
                    dve.wait_ge(res_psum[D_], n.before(D_))
                for w in range(NW):
                    last = v.scalar_tensor_tensor(out=mixed[:, b * 128 + w * WS:b * 128 + (w + 1) * WS],
                                                  in0=bank[3][:, w * WS:(w + 1) * WS], scalar=pl("window", w, 1),
                                                  in1=inv_sum[:, w * WS:(w + 1) * WS], op0=ALU.mult, op1=ALU.mult)
                last.then_inc(u_made, 1)

            def expert_out(n, it, s, j):
                dve.wait_ge(e_taken[j % 2], n(E_, 4, j // 2 + 1))
                v.tensor_tensor(pair_out[j % 4][:, :], pair_out[j % 4][:, :], bank[6][:, 0:N], ALU.mult)\
                    .then_inc(e_weighted[j % 2], 1)

            def residual(n, it, s, k):
                dve.wait_ge(moe_turned, n(E_))
                halves = bank[4][tok, :].rearrange("p (b c f) -> p b c f", b=G, c=2)
                v.tensor_tensor(per_seq(y_res[tok, :]), halves[:, :, 0, :], per_seq(normed[E_][tok, :]), ALU.add)
                settle()
                v.tensor_tensor(per_seq(y_res[tok, :]), halves[:, :, 1, :], per_seq(y_res[tok, :]), ALU.add)
                settle()

            def center2(n, it, s, k):
                center_of(n, E_ + 1, per_seq(y_res[tok, :]))

            def variance2(n, it, s, k):
                variance(n, it, E_ + 1, k)

            def normalise2(n, it, s, k):
                y = E_ + 1
                dve.wait_ge(ln_rstd[y], n(E_))
                v.tensor_tensor(per_seq(normed[y][tok, :]), per_seq(centered[y][tok, :]), over_f(rstd[y][tok, :]), ALU.mult)
                settle()
                v.tensor_tensor(per_seq(normed[y][tok, :]), per_seq(normed[y][tok, :]), over_b(pl("gamma", rows=tok), F), ALU.mult)
                settle()
                v.tensor_tensor(per_seq(normed[y][tok, :]), per_seq(normed[y][tok, :]), over_b(pl("beta", rows=tok), F), ALU.add)
                settle()
                dve.wait_ge(out_stored, n(E_, 16, 0))
                v.nop()
                v.tensor_tensor(y_out[tok, :], normed[y][tok, :], hg(it, E_), ALU.add).then_inc(out_made, 1)

            run(dve, "dve", {"center": center, "variance": variance, "normalise": normalise, "conv_load": conv_load,
                             "conv": conv, "conv_fold": conv_fold, "conv_out": conv_out,
                             "omega": omega_step, "r_out": r_out, "gate": gate, "soft": soft, "top": top,
                             "weights": weights, "h2": h2, "score": score, "mix": mix,
                             "expert_out": expert_out, "residual": residual,
                             "center2": center2, "variance2": variance2, "normalise2": normalise2})

        @block.gpsimd
        def _(pool):
            g = nc.gpsimd
            for t in (x_sq, keys[0], keys[1], q_bd, k_win, v_bd, w_feats[C_], w_feats[E_]):
                g.memset(t[:, :].bitcast(F32) if t.dtype == F32R else t[:, :], 0.0)
            g.memset(minus_half[:, :], -0.5)
            g.memset(half[:, :], 0.5)
            g.memset(eps_tile[:, :], EPS)
            g.drain().then_inc(setup_done, 1)

            def variance(n, it, s, k):
                y = norm_of(s)
                pool.wait_ge(ln_var[y], n(min(s, E_)))
                g.tensor_tensor(var_eps[y][tok, :], var[y][tok, :], eps_tile[tok, :], ALU.add)
                g.drain()
                g.tensor_tensor(rstd[y][tok, :], var_eps[y][tok, :], minus_half[tok, :], ALU.pow).then_inc(ln_rstd[y], 1)

            def normalise(n, it, s, k):
                y = norm_of(s)
                pool.wait_ge(parts_hi[y], n(s))
                p = parts[y][tok, :].rearrange("p (b c f) -> p b c f", b=G, c=2)
                g.tensor_tensor(p[:, :, 1, :], per_seq(normed[y][tok, :]), p[:, :, 0, :].bitcast(F32), ALU.subtract)\
                    .then_inc(parts_lo[y], 1)

            def conv(n, it, s, k):
                pool.wait_ge(energy_read, n(A_))
                g.tensor_tensor(norm[tok, :], energy[tok, :], half[tok, :], ALU.pow).then_inc(norm_made, 1)

            def weights(n, it, s, k):
                pool.wait_ge(w_hi_made[s], n(s))
                p = w_parts[s][tok, :].rearrange("p (b c e) -> p b c e", b=G, c=2)
                g.tensor_tensor(p[:, :, 1, :], weight[s][tok, :].rearrange("p (b e) -> p b e", b=G),
                                p[:, :, 0, :].bitcast(F32), ALU.subtract).then_inc(w_lo_made[s], 1)

            def window_k(n, it, s, k):
                pool.wait_ge(wk_made, n(D_))
                pool.wait_ge(s_psum, n(D_, 4, 0))
                for b in range(G):
                    last = g.tensor_tensor(k_head[:, b * 512:(b + 1) * 512].rearrange("f (h k) -> f h k", h=NH1),
                                           k_win[:, b * WS:(b + 1) * WS].unsqueeze(1).to_broadcast([128, NH1, WS]),
                                           pl("head").unsqueeze(2).to_broadcast([128, NH1, WS]), ALU.mult)
                last.then_inc(k_masked, 1)

            def expert_out(n, it, s, j):
                if j == 0:
                    return
                pool.wait_ge(e_weighted[j % 2], n(E_, 4, j // 2 + 1))
                if j == 1:
                    pool.wait_ge(e_weighted[0], n(E_, 4, 1))
                    pool.wait_ge(moe_turned, n.before(E_))
                    g.tensor_tensor(moe[:, :], pair_out[0][:, :], pair_out[1][:, :], ALU.add).then_inc(e_added[0], 1)
                    g.drain().then_inc(e_added[1], 1)
                else:
                    g.tensor_tensor(moe[:, :], moe[:, :], pair_out[j % 4][:, :], ALU.add).then_inc(e_added[j % 2], 1)
                    if j < E1 // 2 - 1:
                        g.drain()

            def variance2(n, it, s, k):
                variance(n, it, E_ + 1, k)

            run(pool, "pool", {"variance": variance, "normalise": normalise, "conv": conv, "weights": weights,
                               "window_k": window_k, "expert_out": expert_out, "variance2": variance2})


def _stack(w):
    return np.concatenate([w, w], axis=0)


def _layout(i):
    f = np.float32
    s = np.zeros((128, NSPLIT), f)
    p = np.zeros((128, NPLAIN), f)
    e = np.zeros((128, NEXACT), f)

    def put(to, at, name, a, col=0, row=0):
        a = np.asarray(a, f)
        assert col + a.shape[1] <= at[name][1]
        c = at[name][0] + col
        to[row:row + a.shape[0], c:c + a.shape[1]] = a

    k = i["L0_tok_kernel"]
    for t in range(TAPS):
        put(s, SPLIT_AT, "conv", k[t], (t // 2) * 128 + (64 if t % 2 or t == TAPS - 1 else 0))
    for h in range(NH0):
        q = i["L0_attn_Q"][h]
        put(s, SPLIT_AT, "q0", _stack(q), h * F)
        put(p, PLAIN_AT, "e0", i["L0_attn_E"][h].T, (h // 2) * F, 64 * (h % 2))
    for x in range(E0):
        put(s, SPLIT_AT, "w1c", _stack(i["L0_ffn_eW1"][x]), x * 128)
        put(p, PLAIN_AT, "w2c", i["L0_ffn_eW2"][x], x * F)
        put(p, PLAIN_AT, "w3c", i["L0_ffn_eW3"][x], (x // 2) * F, 64 * (x % 2))
        put(p, PLAIN_AT, "b1c", i["L0_ffn_eb1"][x][:, None], x)
        put(p, PLAIN_AT, "b2c", i["L0_ffn_eb2"][x][:, None], x // 2, 64 * (x % 2))
        for part in range(2):
            e[part * E0 + x, EXACT_AT["sel_c"][0] + x * F:EXACT_AT["sel_c"][0] + (x + 1) * F] = 1
    put(s, SPLIT_AT, "w1c", _stack(i["L0_ffn_sW1"]), E0 * 128)
    put(p, PLAIN_AT, "b1c", i["L0_ffn_sb1"][:, None], E0)
    put(p, PLAIN_AT, "w2s", i["L0_ffn_sW2"])
    put(p, PLAIN_AT, "b2c", i["L0_ffn_sb2"][:, None], 2)
    put(p, PLAIN_AT, "w3c", i["L0_ffn_sW3"], 2 * F)
    put(p, PLAIN_AT, "b3c", np.tile(i["L0_ffn_sb3"], 2)[:, None])
    put(p, PLAIN_AT, "eb3", _stack(i["L0_ffn_eb3"]))
    put(p, PLAIN_AT, "gwc", _stack(i["L0_ffn_gW"]))
    qkv = i["L1_attn_w_qkv"]
    put(s, SPLIT_AT, "wq", _stack(np.tile(qkv[0:64].T, (1, 2))))
    put(s, SPLIT_AT, "wk", _stack(np.tile(qkv[64:128].T, (1, 2))))
    put(p, PLAIN_AT, "wv", _stack(np.tile(qkv[128:192].T, (1, 2))))
    put(p, PLAIN_AT, "fold", np.tile(np.eye(64), (2, 2)))
    wp = i["L1_attn_w_proj"].T.reshape(4, 1, 2, HD, F)
    put(p, PLAIN_AT, "wp", np.tile(wp, (1, 2, 1, 1, 1)).reshape(128, F))
    put(p, PLAIN_AT, "bp", np.tile(i["L1_attn_b_proj"], 2)[:, None])
    pos = np.arange(WS)
    rel = i["L1_attn_rel_bias"][pos[None, :] - pos[:, None] + WS - 1]
    put(e, EXACT_AT, "rel", _stack(np.tile(rel, (1, NH1))))
    put(e, EXACT_AT, "query", np.tile(np.eye(WS), (2, 2)))
    for x in range(E1):
        put(s, SPLIT_AT, "w1e", _stack(i["L1_ffn_w1"][x]), x * 128)
        put(p, PLAIN_AT, "w2e", i["L1_ffn_w2"][x], x * F)
        put(p, PLAIN_AT, "b1e", i["L1_ffn_b1"][x][:, None], x)
        for part in range(2):
            e[part * E1 + x, EXACT_AT["sel_e"][0] + x * F:EXACT_AT["sel_e"][0] + (x + 1) * F] = 1
        put(p, PLAIN_AT, "b2e", i["L1_ffn_b2"][x][:, None], x // 2, 64 * (x % 2))
    put(p, PLAIN_AT, "gwe", _stack(i["L1_ffn_gate_w"]))
    row = {"bias_conv": i["L0_tok_bias"], "gbc": i["L0_ffn_gb"], "gbe": i["L1_ffn_gate_b"], "gamma": i["L1_ffn_gamma"],
           "beta": i["L1_ffn_beta"], "alpha": i["L0_tok_alpha"].reshape(1), "tau": i["L0_tok_tau"].reshape(1),
           "scale": i["L0_tok_scale"].reshape(1), "rank_c": np.arange(E0, 0, -1), "rank_e": np.arange(E1, 0, -1)}
    for name, a in row.items():
        put(p, PLAIN_AT, name, np.tile(np.asarray(a)[None, :], (128, 1)))
    put(p, PLAIN_AT, "ident", np.eye(128))
    u, t = np.arange(128)[:, None], np.arange(L)[None, :]
    put(p, PLAIN_AT, "causal", u <= t)
    put(p, PLAIN_AT, "band", (u >= t) & (u < t + TAPS))
    r = np.arange(128)
    c = np.arange(32)
    put(p, PLAIN_AT, "ones_bd", (r[:, None] // 64) == (c[None, :] // 8) % 2)
    put(p, PLAIN_AT, "window", ((r[:, None] // 16) % 2) == np.arange(2)[None, :])
    put(p, PLAIN_AT, "head", ((r[:, None] % 64) // HD) == np.arange(NH1)[None, :])
    return s, p, e


def kernel(**inputs):
    import concourse.bacc as bacc
    from concourse.bass_utils import run_bass_kernel_spmd

    i = {k: np.asarray(a) for k, a in inputs.items()}
    s, p, e = _layout(i)
    nc = bacc.Bacc("TRN2", target_bir_lowering=False, num_devices=1)
    arrays = {"x_dram": np.ascontiguousarray(i["x"]), "split_dram": s, "plain_dram": p, "exact_dram": e}
    args = [nc.dram_tensor(name, a.shape, F32, kind="ExternalInput").ap() for name, a in arrays.items()]
    out = nc.dram_tensor("out_dram", (B, L, F), F32, kind="ExternalOutput").ap()
    tower(nc, *args, out)
    r = run_bass_kernel_spmd(nc, [arrays], core_ids=[0])
    return r.results[0]["out_dram"]
```
